# Optimizing a Trainium2 kernel written in Bass

```python
import numpy as np
import jax
import jax.numpy as jnp

def _softmax(x, axis=-1):
    return jax.nn.softmax(x, axis=axis)

def _gelu(x):
    return jax.nn.gelu(x, approximate=True)

def _silu(x):
    return jax.nn.silu(x)

def _sigmoid(x):
    return jax.nn.sigmoid(x)

def _layernorm(x, axis=-1, eps=1e-05):
    m = jnp.mean(x, axis=axis, keepdims=True)
    v = jnp.var(x, axis=axis, keepdims=True)
    return (x - m) / jnp.sqrt(v + eps)

def _scatter_add(tgt, idx, src, axis=0):
    return tgt.at[idx].add(src)

def _segment_sum(src, seg, n):
    return jax.ops.segment_sum(src, seg, n)
kernel_name = 'mk_metaformer_d1_conv_nhwc256_r4_10b186'

def setup_inputs(seed: int=0):
    np.random.seed(seed)
    _w = jnp.asarray

    def _rec_inputs():
        import jax
        import jax.numpy as jnp
        _gk = jax.random.key(seed)
        x = -0.000125 + 0.9999 * jax.random.normal(jax.random.fold_in(_gk, 1), (32, 16, 16, 64), jnp.float32)
        return x
    x = _rec_inputs()

    def _L0_conv_setup():
        import jax, jax.numpy as jnp
        import numpy as np
        from jax import lax
        HEADS, DK, DV, WSZ = (8, 32, 32, 8)
        SCALE = DK ** (-0.5)

        def _conv(t, w):
            return lax.conv_general_dilated(t, w, (1, 1), 'SAME', dimension_numbers=('NHWC', 'HWIO', 'NHWC'))
        key = jax.random.key(seed)
        ks = jax.random.split(key, 8)
        B, H, W, C = (32, 16, 16, 64)
        s1 = 1.0 / np.sqrt(C)
        s3 = 1.0 / np.sqrt(9 * C)
        return {'x': jax.random.normal(ks[0], (B, H, W, C), jnp.float32), 'w_q': jax.random.normal(ks[1], (1, 1, C, DK * HEADS), jnp.float32) * s1, 'w_k': jax.random.normal(ks[2], (1, 1, C, DK * HEADS), jnp.float32) * s1, 'w_v': jax.random.normal(ks[3], (1, 1, C, DV * HEADS), jnp.float32) * s1, 'w_local': jax.random.normal(ks[4], (3, 3, DV * HEADS, DV * HEADS), jnp.float32) * s3, 'b_local': jnp.zeros((DV * HEADS,), jnp.float32), 'w_out': jax.random.normal(ks[5], (1, 1, DV * HEADS, C), jnp.float32) * s1, 'b_out': jnp.zeros((C,), jnp.float32)}
    _L0_conv_all = _L0_conv_setup()
    _L0_conv_in = {k: v for k, v in _L0_conv_all.items() if k in ('w_q', 'w_k', 'w_v', 'w_local', 'b_local', 'w_out', 'b_out')}
    del _L0_conv_all

    def _L0_ffn_setup():
        import jax, jax.numpy as jnp
        import numpy as np
        TOP_K = 2
        key = jax.random.key(seed)
        ks = jax.random.split(key, 4)
        B, L, D, H, E = (8, 1024, 64, 256, 8)
        s = 0.02
        return {'x': jax.random.normal(ks[0], (B, L, D), jnp.float32), 'Wg': jax.random.normal(ks[1], (D, E), jnp.float32) * s, 'bg': jnp.zeros((E,), jnp.float32), 'W1': jax.random.normal(ks[2], (E, D, H), jnp.float32) * s, 'b1': jnp.zeros((E, H), jnp.float32), 'W2': jax.random.normal(ks[3], (E, H, D), jnp.float32) * s, 'b2': jnp.zeros((E, D), jnp.float32)}
    _L0_ffn_all = _L0_ffn_setup()
    _L0_ffn_in = {k: v for k, v in _L0_ffn_all.items() if k in ('Wg', 'bg', 'W1', 'b1', 'W2', 'b2')}
    del _L0_ffn_all
    return {'x': x, 'L0_conv_w_q': _L0_conv_in['w_q'], 'L0_conv_w_k': _L0_conv_in['w_k'], 'L0_conv_w_v': _L0_conv_in['w_v'], 'L0_conv_w_local': _L0_conv_in['w_local'], 'L0_conv_b_local': _L0_conv_in['b_local'], 'L0_conv_w_out': _L0_conv_in['w_out'], 'L0_conv_b_out': _L0_conv_in['b_out'], 'L0_ffn_Wg': _L0_ffn_in['Wg'], 'L0_ffn_bg': _L0_ffn_in['bg'], 'L0_ffn_W1': _L0_ffn_in['W1'], 'L0_ffn_b1': _L0_ffn_in['b1'], 'L0_ffn_W2': _L0_ffn_in['W2'], 'L0_ffn_b2': _L0_ffn_in['b2']}

def reference(x, L0_conv_w_q, L0_conv_w_k, L0_conv_w_v, L0_conv_w_local, L0_conv_b_local, L0_conv_w_out, L0_conv_b_out, L0_ffn_Wg, L0_ffn_bg, L0_ffn_W1, L0_ffn_b1, L0_ffn_W2, L0_ffn_b2):
    import jax
    import jax.numpy as jnp

    def _L0_conv_ref(x, w_q, w_k, w_v, w_local, b_local, w_out, b_out):
        import jax, jax.numpy as jnp
        import numpy as np
        from jax import lax
        HEADS, DK, DV, WSZ = (8, 32, 32, 8)
        SCALE = DK ** (-0.5)

        def _conv(t, w):
            return lax.conv_general_dilated(t, w, (1, 1), 'SAME', dimension_numbers=('NHWC', 'HWIO', 'NHWC'))
        B, H, W, C = x.shape
        nx, ny = (H // WSZ, W // WSZ)
        q = _conv(x, w_q)
        k = _conv(x, w_k)
        v = _conv(x, w_v)
        local_out = _conv(v, w_local) + b_local

        def to_windows(t, d):
            t = t.reshape(B, nx, WSZ, ny, WSZ, HEADS, d)
            return t.transpose(0, 1, 3, 5, 2, 4, 6).reshape(B * nx * ny, HEADS, WSZ * WSZ, d)
        qw, kw, vw = (to_windows(q, DK), to_windows(k, DK), to_windows(v, DV))
        dots = jnp.einsum('bhid,bhjd->bhij', qw, kw) * SCALE
        attn = jax.nn.softmax(dots, axis=-1)
        out = jnp.einsum('bhij,bhjd->bhid', attn, vw)
        out = out.reshape(B, nx, ny, HEADS, WSZ, WSZ, DV)
        out = out.transpose(0, 1, 4, 2, 5, 3, 6).reshape(B, H, W, HEADS * DV)
        out = out + local_out
        out = _conv(out, w_out) + b_out
        return out

    def _L0_ffn_ref(x, Wg, bg, W1, b1, W2, b2):
        import jax, jax.numpy as jnp
        import numpy as np
        TOP_K = 2
        B, L, D = x.shape
        E = W1.shape[0]
        xf = x.reshape(-1, D)
        gate_logits = xf @ Wg + bg
        top_w, top_i = jax.lax.top_k(gate_logits, TOP_K)
        top_w = jax.nn.softmax(top_w, axis=-1)
        w_dense = jnp.sum(jax.nn.one_hot(top_i, E, dtype=xf.dtype) * top_w[..., None], axis=1)
        out = jnp.zeros_like(xf)
        for e in range(E):
            h = jax.nn.gelu(xf @ W1[e] + b1[e], approximate=False)
            out = out + w_dense[:, e:e + 1] * (h @ W2[e] + b2[e])
        return out.reshape(B, L, D)

    def _gn(v, G=32, eps=1e-05):
        B_, H_, W_, C_ = v.shape
        g = v.reshape(B_, H_, W_, G, C_ // G)
        m = jnp.mean(g, axis=(1, 2, 4), keepdims=True)
        s = jnp.var(g, axis=(1, 2, 4), keepdims=True)
        return ((g - m) / jnp.sqrt(s + eps)).reshape(v.shape)

    def _ln_c(v, eps=1e-06):
        m = jnp.mean(v, axis=-1, keepdims=True)
        s = jnp.var(v, axis=-1, keepdims=True)
        return (v - m) / jnp.sqrt(s + eps)

    def _ln_t(v, eps=1e-05):
        m = jnp.mean(v, axis=-1, keepdims=True)
        s = jnp.var(v, axis=-1, keepdims=True)
        return (v - m) / jnp.sqrt(s + eps)

    def _to_tokens(v):
        B_, H_, W_, C_ = v.shape
        return v.reshape(B_, H_ * W_, C_)

    def _from_tokens(t, like):
        return t.reshape(like.shape)
    x = x + _L0_conv_ref(_ln_c(x), L0_conv_w_q, L0_conv_w_k, L0_conv_w_v, L0_conv_w_local, L0_conv_b_local, L0_conv_w_out, L0_conv_b_out)
    t = _to_tokens(x)
    t = t + _L0_ffn_ref(_ln_t(t), L0_ffn_Wg, L0_ffn_bg, L0_ffn_W1, L0_ffn_b1, L0_ffn_W2, L0_ffn_b2)
    x = _from_tokens(t, x)
    return x

_drawn_inputs = setup_inputs


def setup_inputs(seed=0):
    import zlib

    import numpy as np

    out = dict(_drawn_inputs(seed))
    spreads = {'L0_conv_b_local': (0.0, 0.1),
     'L0_conv_b_out': (0.0, 0.34),
     'L0_ffn_bg': (0.0, 0.654),
     'L0_ffn_b1': (0.0, 0.8),
     'L0_ffn_b2': (0.0, 0.492)}
    factors = {'L0_ffn_Wg': 3.725, 'L0_ffn_W1': 8.0, 'L0_ffn_W2': 8.0}
    for name, (base, spread) in spreads.items():
        noise = np.random.default_rng([zlib.crc32(name.encode()), seed]).standard_normal(out[name].shape)
        drawn = base * np.exp(spread * noise) if base else spread * noise
        out[name] = jnp.asarray(drawn.astype(out[name].dtype))
    for name, factor in factors.items():
        out[name] = (out[name] * factor).astype(out[name].dtype)
    return out
```

```python
import numpy as np

import concourse.bass as bass
from concourse import mybir
from contextlib import ExitStack

F32 = mybir.dt.float32
F16 = mybir.dt.float16
U32 = mybir.dt.uint32
ACT = mybir.ActivationFunctionType
ALU = mybir.AluOpType
AX = mybir.AxisListType

B, HI, WI, C = 32, 16, 16, 64
HEADS, DK, WSZ = 8, 32, 8
HC = HEADS * DK
E, HID = 8, 256
P = 128
WT = WSZ * WSZ
NT = B * HI * WI // P
TG = 4
NG = NT // TG
GT = TG * P
IG = GT // (HI * WI)
PAIRS = HEADS // 2
EP = E // 2
TAPS = 9
PADW = WI + 2
CH = E * HID // P
EPS_C, EPS_T = 1e-6, 1e-5
SCALE = DK ** -0.5
XS = 16.0
WS = 16.0


def at(g, per, extra):
    i, off = g
    static = off * per + extra
    return static if i is None else i * (2 * per) + static


def sh(g, d):
    return (g[0], g[1] + d)


def real(g):
    return g[0] is not None or 0 <= g[1] < NG


def is_first(g):
    return g[0] is None and g[1] == 0


def tile(g, u):
    return sh(g, u // TG), u % TG


def idx(g, per, extra=0):
    return at(g, per, extra)


def wait(eng, sem, value):
    if isinstance(value, int) and value <= 0:
        return
    eng.wait_ge(sem, value)


def steps(eng, body, first, last):
    for s in range(first, 4):
        body((None, s))
    with eng.Fori(2, NG // 2 - 1) as i:
        body((i, 0))
        body((i, 1))
    for s in range(NG - 2, last + 1):
        body((None, s))


def expert(c):
    return 2 * (c // 4) + c % 2, (c % 4) // 2


GATE = 21


def program(nc, x, w_q, w_k, w_v, w_local, b_local, w_out, b_out, wg, bg, w1, b1, w2, b2, out):
    ctx = ExitStack()
    with ctx:
        def sb(name, shape, dt=F32):
            return ctx.enter_context(nc.sbuf_tensor(name, shape, dt))

        def sem(name):
            return ctx.enter_context(nc.semaphore(name))

        ident = sb("ident", [P, P])
        ident16 = sb("ident16", [P, P], F16)
        iota8 = sb("iota8", [P, E])
        sel = sb("sel", [2 * E, EP, P], F16)
        wq_sb = sb("wq_sb", [C, HC])
        wk_sb = sb("wk_sb", [C, HC])
        wv_sb = sb("wv_sb", [C, HC])
        wqT = sb("wqT", [DK, HEADS, 2, C])
        wkT = sb("wkT", [DK, HEADS, C])
        wvTh = sb("wvTh", [DK, HEADS, C])
        wvT = sb("wvT", [P, 2, 2, C])
        wloc = sb("wloc", [P, 2, TAPS, HC])
        wo_sb = sb("wo_sb", [P, 2, C])
        wo_h = sb("wo_h", [DK, HEADS, C])
        vlT = sb("vlT", [P, TAPS, 2, P])
        rows = sb("rows", [23, P])
        cols = sb("cols", [P, 23])
        ybias = sb("ybias", [P, 1])
        bg_sb = sb("bg_sb", [P, E])
        g32 = sb("g32", [P, HEADS * C])
        g_hi = sb("g_hi", [P, HEADS * C], F16)
        g_lo = sb("g_lo", [P, HEADS * C], F16)
        cv32 = sb("cv32", [P, TAPS * C])
        cv = sb("cv", [P, TAPS, 2, C], F16)
        wvo = sb("wvo", [P, PAIRS, C])
        w1_sb = sb("w1_sb", [P, E * HID])
        w1_hi = sb("w1_hi", [P, E * HID], F16)
        w1_lo = sb("w1_lo", [P, E * HID], F16)
        wg_sb = sb("wg_sb", [P, E])
        wg_hl = sb("wg_hl", [P, 2, E], F16)
        w2_sb = sb("w2_sb", [P, E, 2, C])
        x_sb = sb("x_sb", [P, NT, C])
        x1 = sb("x1", [P, NT, C])
        st = sb("st", [P, NT, 6])
        mean = sb("mean", [P, NT])
        rstd = sb("rstd", [P, NT])
        va = sb("va", [P, NT])
        vb = sb("vb", [P, NT])
        vc = sb("vc", [P, NT])
        xn = sb("xn", [P, 2, TG, 2, C])
        hl = sb("hl", [P, 2, TG, 2, C], F16)
        xsp = sb("xsp", [P, 2, IG, PADW, PADW], F16)
        bd = sb("bd", [P, 2, TG * 2, 2, WT])
        bt = sb("bt", [P, 2, TG * 2, P])
        aa = sb("aa", [P, 2, PAIRS, GT])
        sc = sb("sc", [P, 2, HEADS, WT])
        pe_ = sb("pe_", [P, 2, HEADS, WT])
        pn = sb("pn", [P, 2, HEADS * WT])
        pt = sb("pt", [P, 2, PAIRS, P])
        mx = sb("mx", [P, 2, HEADS])
        sm = sb("sm", [P, 2, HEADS])
        rs = sb("rs", [P, 2, HEADS])
        zs = sb("zs", [P, 2, TG, PAIRS, P])
        ys = sb("ys", [P, 2, GT])
        tmp = sb("tmp", [P, 2, TG, C])
        xs2 = sb("xs2", [P, 2, GT], F16)
        lg = sb("lg", [P, 2, TG, E])
        top = sb("top", [P, 2, TG, 8])
        topi = sb("topi", [P, 2, TG, 8], U32)
        topf = sb("topf", [P, 2, TG, 2])
        gap = sb("gap", [P, 2, TG])
        th = sb("th", [P, 2, TG])
        w12 = sb("w12", [P, 2, TG, 2])
        oh = sb("oh", [P, 2, 2, TG, E])
        wd = sb("wd", [P, 2, TG, E])
        wdh = sb("wdh", [P, 2, TG, 2, E], F16)
        wdT = sb("wdT", [2 * E, 2, GT], F16)
        wb = zs[:].rearrange("p b t a c -> p b t (a c)")
        wl = wloc[:].rearrange("p k t o -> p k (t o)")
        hh = wl[:, 0, 0:4 * GT].rearrange("p (a b) -> p a b", a=4)
        yw = wl[:, 1, 0:EP * GT].rearrange("p (a b) -> p a b", a=EP)
        acc = sb("acc", [P, 2, GT])
        ob = sb("ob", [P, 2, TG, C])

        banks = [ctx.enter_context(nc.psum_tensor(f"bank{i}", [P, 512], F32)) for i in range(8)]

        wts = sem("wts")
        wts2 = sem("wts2")
        wlocs = sem("wlocs")
        ffnw = sem("ffnw")
        xl = [sem(f"xl{i}") for i in range(4)]
        idn = sem("idn")
        prep_pe = sem("prep_pe")
        prep_cp = sem("prep_cp")
        dself = sem("dself")
        pself = sem("pself")
        aself = sem("aself")
        w1_ready = sem("w1_ready")
        sq_in = sem("sq_in")
        sq_done = sem("sq_done")
        zeroed = sem("zeroed")
        norm_ready = sem("norm_ready")
        x16_done = sem("x16_done")
        xt32_done = sem("xt32_done")
        xsp_ready = sem("xsp_ready")
        bd_ready = sem("bd_ready")
        a_done = sem("a_done")
        a_ready = sem("a_ready")
        bt_done = sem("bt_done")
        bt_ready = sem("bt_ready")
        dots_done = sem("dots_done")
        mx_ready = sem("mx_ready")
        sub_ready = sem("sub_ready")
        exp_ready = sem("exp_ready")
        sum_ready = sem("sum_ready")
        rs_ready = sem("rs_ready")
        pn_ready = sem("pn_ready")
        pt_done = sem("pt_done")
        pt_ready = sem("pt_ready")
        z_done = sem("z_done")
        z_ready = sem("z_ready")
        conv_done = sem("conv_done")
        att_done = sem("att_done")
        y_ready = sem("y_ready")
        yt_done = sem("yt_done")
        x1_ready = sem("x1_ready")
        half_ready = sem("half_ready")
        st_ready = sem("st_ready")
        xt2_done = sem("xt2_done")
        xs2_ready = sem("xs2_ready")
        gate_done = sem("gate_done")
        gate_step = sem("gate_step")
        tanh_ready = sem("tanh_ready")
        wt_done = sem("wt_done")
        wt_ready = sem("wt_ready")
        wb_done = sem("wb_done")
        wb_ready = sem("wb_ready")
        h_done = sem("h_done")
        gelu_ready = sem("gelu_ready")
        ffn2_done = sem("ffn2_done")
        yw_ready = sem("yw_ready")
        acc_ready = sem("acc_ready")
        f_done = sem("f_done")
        o_step = sem("o_step")
        out_ready = sem("out_ready")
        stored = [sem(f"stored{i}") for i in range(2)]

        block = ctx.enter_context(nc.Block())

        x_tiles = x.rearrange("(t p) d -> p t d", p=P)
        out_tiles = out.rearrange("(t p) d -> p t d", p=P)

        dots = [banks[0], banks[1]]
        ptb, zb = banks[2], banks[3]
        outb = [banks[4], banks[5]]
        ring = [banks[6], banks[7]]
        hidb = [banks[i] for i in range(4)]

        def half(bank):
            return bank[:, 0:256].bitcast(F16)

        @block.sync
        def _(sp):
            QT = NT // 4
            sp.dma_start(wq_sb[:], w_q[0, 0]).then_inc(wts, 16)
            sp.dma_start(wk_sb[:], w_k[0, 0]).then_inc(wts, 16)
            sp.dma_start(wv_sb[:], w_v[0, 0]).then_inc(wts, 16)
            for q in range(4):
                sp.dma_start(x_sb[:, q * QT:(q + 1) * QT, :], x_tiles[:, q * QT:(q + 1) * QT, :]).then_inc(xl[q], 16)
            for k in range(2):
                sp.dma_start(wloc[:, k], w_local.rearrange("a b i o -> i (a b) o")[k * P:(k + 1) * P]).then_inc(wlocs, 16)

            def body(g):
                prv = sh(g, -1)
                if real(prv):
                    b = prv[1] % 2
                    wait(sp, out_ready, at(prv, 1, 1))
                    sp.dma_start(out_tiles[:, bass.ds(idx(prv, TG), TG), :], ob[:, b]).then_inc(stored[b], 16)
            steps(sp, body, 0, NG)
            for b in range(2):
                sp.wait_ge(stored[b], 16 * (NG // 2))

        @block.gpsimd
        def _(pool):
            nc.gpsimd.memset(ident[:], 0.0).then_inc(pself, 1)
            nc.gpsimd.iota(iota8[:], [[1, E]], base=0, channel_multiplier=0,
                           allow_small_or_imprecise_dtypes=True).then_inc(idn, 1)
            pool.wait_ge(pself, 1)
            nc.gpsimd.affine_select(out=ident[:], in_=ident[:], compare_op=ALU.not_equal, fill=1.0, base=0,
                                    pattern=[[-1, P]], channel_multiplier=1).then_inc(idn, 1)
            pool.wait_ge(idn, 2)
            nc.gpsimd.tensor_copy(ident16[:], ident[:]).then_inc(idn, 1)
            nc.gpsimd.memset(xsp[:], 0.0).then_inc(zeroed, 1)
            nc.gpsimd.memset(bd[:], 0.0).then_inc(zeroed, 1)
            pool.wait_ge(w1_ready, 2)
            nc.gpsimd.tensor_tensor(w1_lo[:], w1_sb[:], w1_hi[:], ALU.subtract).then_inc(w1_ready, 1)

            def body(g):
                for u in range(TG):
                    t, v = tile(g, u)
                    if not real(t):
                        continue
                    wait(pool, rs_ready, at(t, TG, v + 1))
                    wait(pool, pt_done, at(t, TG, v - 1))
                    nc.gpsimd.tensor_tensor(pn[:, v % 2, :].rearrange("p (h j) -> p h j", h=HEADS), pe_[:, v % 2],
                                            rs[:, v % 2].unsqueeze(2).broadcast_to([P, HEADS, WT]),
                                            ALU.mult).then_inc(pn_ready, 1)
            steps(pool, body, 0, NG - 1)

            def experts(g):
                if not real(g):
                    return
                b = g[1] % 2
                wait(pool, f_done, at(g, 1, -1))
                wait(pool, yw_ready, at(g, EP, 2))
                nc.gpsimd.tensor_tensor(acc[:, b], yw[:, 0], yw[:, 1], ALU.add).then_inc(acc_ready, 1)
                for p in (2, 3):
                    wait(pool, yw_ready, at(g, EP, p + 1))
                    wait(pool, acc_ready, at(g, 3, p - 1))
                    nc.gpsimd.tensor_tensor(acc[:, b], acc[:, b], yw[:, p], ALU.add).then_inc(acc_ready, 1)
            steps(pool, experts, 0, NG - 1)

        @block.scalar
        def _(act):
            act.dma_start(wo_sb[:], w_out[0, 0].rearrange("(k i) o -> i k o", i=P)).then_inc(wts2, 16)
            act.dma_start(wo_h[:], w_out[0, 0].rearrange("(h d) o -> d h o", d=DK)).then_inc(wts2, 16)
            act.dma_start(rows[0:16, :], b1.rearrange("e (k n) -> (e k) n", n=P)).then_inc(wts2, 16)
            act.dma_start(rows[16:20, :], b2.rearrange("(p e) n -> p (e n)", e=2)).then_inc(wts2, 16)
            act.dma_start(rows[20:22, :], b_local.rearrange("(k n) -> k n", n=P)).then_inc(wts2, 16)
            act.dma_start(rows[22:23, 0:C], b_out.unsqueeze(0)).then_inc(wts2, 16)
            act.dma_start(rows[22:23, C:P], b_out.unsqueeze(0)).then_inc(wts2, 16)
            act.dma_start(bg_sb[:], bg.unsqueeze(0).broadcast_to([P, E])).then_inc(ffnw, 16)
            for h in range(2):
                act.dma_start(w1_sb[h * C:(h + 1) * C, :].rearrange("c (e n) -> c e n", e=E),
                              w1.rearrange("e c n -> c e n")).then_inc(ffnw, 16)
                act.dma_start(wg_sb[h * C:(h + 1) * C, :], wg).then_inc(ffnw, 16)
            act.dma_start(w2_sb[:], w2.rearrange("e (k n) c -> n e k c", n=P)).then_inc(ffnw, 16)

            act.wait_ge(prep_pe, 1)
            nc.scalar.copy(wkT[:], banks[1][0:DK, :].rearrange("p (h c) -> p h c", h=HEADS)).then_inc(prep_cp, 1)
            nc.scalar.copy(wvTh[:], banks[2][0:DK, :].rearrange("p (h c) -> p h c", h=HEADS)).then_inc(prep_cp, 1)
            act.wait_ge(ffnw, 16 * 6)
            nc.scalar.mul(w1_sb[:], w1_sb[:], WS).then_inc(w1_ready, 1)
            act.wait_ge(w1_ready, 1)
            nc.scalar.copy(w1_hi[:], w1_sb[:]).then_inc(w1_ready, 1)
            act.wait_ge(sq_in, 1)
            nc.scalar.sqrt(vb[:], va[:]).then_inc(sq_done, 1)

            def body(g):
                nxt = sh(g, 1)
                for u in range(TG):
                    if real(nxt):
                        if u == 0:
                            wait(act, x16_done, at(nxt, 1, 1))
                            wait(act, conv_done, at(nxt, 1, -1))
                            if is_first(nxt):
                                act.wait_ge(zeroed, 1)
                            b = nxt[1] % 2
                            src = half(ring[nxt[1] % 2])
                            nc.scalar.copy(xsp[:, b, :, 1:1 + HI, 1:1 + WI],
                                           src.rearrange("p (m y c) -> p m y c", m=IG, y=HI)).then_inc(xsp_ready, 1)
                        if u in (1, 2):
                            for pr in (2 * (u - 1), 2 * (u - 1) + 1):
                                wait(act, a_done, at(nxt, PAIRS, pr + 1))
                                wait(act, dots_done, at(nxt, TG, -TG))
                                k = (2, 3, 5, 6)[pr]
                                src = ring[(k + nxt[1]) % 2]
                                dst = aa[:, nxt[1] % 2, pr, :].rearrange("p (n ty c) -> p ty n c", n=2, c=WSZ)
                                nc.scalar.mul(dst, src[:].rearrange("p (ty n c) -> p ty n c", n=2, c=WSZ),
                                              1.0 / WS).then_inc(a_ready, 1)
                    t, v = tile(g, u)
                    if real(t):
                        wait(act, sub_ready, at(t, TG, v + 1))
                        wait(act, pn_ready, at(t, TG, v - 1))
                        wait(act, sum_ready, at(t, TG, v - 1))
                        nc.scalar.activation(pe_[:, v % 2], sc[:, v % 2], ACT.Exp,
                                             scale=SCALE / XS / XS).then_inc(exp_ready, 1)
                    t, v = tile(g, u - 2)
                    if real(t):
                        wait(act, pt_done, at(t, TG, v + 1))
                        wait(act, z_done, at(t, TG, v - 1))
                        nc.scalar.copy(pt[:, v % 2], ptb[:].rearrange("p (a b) -> p a b", a=PAIRS)).then_inc(pt_ready, 1)
                    t, v = tile(g, u - 3)
                    if real(t):
                        wait(act, z_done, at(t, TG, v + 1))
                        wait(act, att_done, at(t, 1, -1))
                        nc.scalar.copy(zs[:, t[1] % 2, v], zb[:].rearrange("p (a b) -> p a b", a=PAIRS)).then_inc(z_ready, 1)
                    prv = sh(g, -1)
                    if u == TG - 1 and real(prv):
                        wait(act, att_done, at(prv, 1, 1))
                        wait(act, yt_done, at(prv, 1, -1))
                        src = outb[prv[1] % 2]
                        nc.scalar.activation(ys[:, prv[1] % 2, :], src[:], ACT.Identity, scale=1.0 / (XS * WS), bias=ybias[:, 0:1]).then_inc(y_ready, 1)
            steps(act, body, -1, NG)

            act.wait_ge(sq_in, 2)
            nc.scalar.sqrt(vb[:], va[:]).then_inc(sq_done, 1)

            def experts(g):
                nxt = sh(g, 1)
                for j in range(CH // 2):
                    if real(g):
                        for c in (2 * j, 2 * j + 1):
                            e, k = expert(c)
                            wait(act, h_done, at(g, CH, c + 1))
                            wait(act, ffn2_done, at(g, CH // 2, (c - 4) // 2 + 1))
                            nc.scalar.activation(hh[:, c % 4], hidb[c % 4][:], ACT.Gelu, scale=1.0 / (XS * WS),
                                                 bias=cols[:, 2 * e + k:2 * e + k + 1]).then_inc(gelu_ready, 1)
                    if j == 3 and real(nxt):
                        wait(act, gate_step, at(nxt, GATE, 7))
                        nc.scalar.activation(th[:, nxt[1] % 2], gap[:, nxt[1] % 2], ACT.Tanh, scale=0.5).then_inc(tanh_ready, 1)
                    if j == 5 and real(nxt):
                        wait(act, wt_done, at(nxt, 1, 1))
                        wait(act, wb_done, at(nxt, EP, -EP))
                        nc.scalar.copy(wdT[:, nxt[1] % 2], half(ring[1])[0:2 * E]).then_inc(wt_ready, 1)
                    if j in (6, 7) and real(nxt):
                        for p in (2 * (j - 6), 2 * (j - 6) + 1):
                            wait(act, wb_done, at(nxt, EP, p + 1))
                            wait(act, yw_ready, at(nxt, EP, -EP))
                            nc.scalar.copy(wb[:, nxt[1] % 2, p], ring[p % 2][:]).then_inc(wb_ready, 1)
            steps(act, experts, -1, NG - 1)

        @block.vector
        def _(dve):
            n = [0]

            def link(ins):
                n[0] += 1
                ins.then_inc(dself, 1)
                dve.wait_ge(dself, n[0])

            def rsqrt(eps, count):
                me, qe, mo, qo = st[:, :, 1], st[:, :, 2], st[:, :, 4], st[:, :, 5]
                link(nc.vector.tensor_tensor(mean[:], me, mo, ALU.add))
                link(nc.vector.tensor_tensor(va[:], me, mo, ALU.subtract))
                link(nc.vector.tensor_tensor(vb[:], qe, qo, ALU.add))
                link(nc.vector.tensor_scalar(mean[:], mean[:], 0.5, None, ALU.mult))
                link(nc.vector.tensor_tensor(va[:], va[:], va[:], ALU.mult))
                link(nc.vector.tensor_scalar(vb[:], vb[:], 1.0 / C, eps, ALU.mult, ALU.add))
                link(nc.vector.scalar_tensor_tensor(vc[:], va[:], 0.25, vb[:], ALU.mult, ALU.add))
                nc.vector.tensor_copy(va[:], vc[:]).then_inc(sq_in, 1)
                dve.wait_ge(sq_done, count)
                link(nc.vector.reciprocal(rstd[:], vb[:]))
                link(nc.vector.tensor_tensor(vb[:], rstd[:], rstd[:], ALU.mult))
                link(nc.vector.tensor_tensor(va[:], vb[:], vc[:], ALU.mult))
                link(nc.vector.tensor_scalar(va[:], va[:], -0.5 * XS, 1.5 * XS, ALU.mult, ALU.add))
                link(nc.vector.tensor_tensor(rstd[:], rstd[:], va[:], ALU.mult))

            dve.wait_ge(prep_pe, 1)
            nc.vector.tensor_copy(wqT[:], banks[0][0:DK, :].rearrange("p (h c) -> p h c", h=HEADS)
                                  .unsqueeze(2).broadcast_to([DK, HEADS, 2, C])).then_inc(prep_cp, 1)
            nc.vector.tensor_copy(wvT[:], banks[3][:, 0:2 * C].rearrange("p (k c) -> p k c", k=2)
                                  .unsqueeze(2).broadcast_to([P, 2, 2, C])).then_inc(prep_cp, 1)
            nc.vector.tensor_copy(cols[:], banks[3][:, 256:256 + 23]).then_inc(prep_cp, 1)
            dve.wait_ge(idn, 3)
            link(nc.vector.tensor_tensor(
                sel[:].rearrange("k p (e c) -> k (p e) c", e=2),
                ident[0:2 * E, 0:E].unsqueeze(2).broadcast_to([2 * E, E, C]),
                ident[0:2 * E, E:2 * E].unsqueeze(2).broadcast_to([2 * E, E, C]), ALU.add))
            dve.wait_ge(prep_pe, 2)
            link(nc.vector.tensor_scalar(g32[:], banks[4][:], WS, None, ALU.mult))
            link(nc.vector.tensor_copy(g_hi[:], g32[:]))
            link(nc.vector.tensor_tensor(g_lo[:], g32[:], g_hi[:], ALU.subtract))
            link(nc.vector.tensor_scalar(wvo[:], banks[5][:, 0:PAIRS * C].rearrange("p (a c) -> p a c", a=PAIRS),
                                         WS, None, ALU.mult))
            link(nc.vector.memset(ybias[:], 0.0))
            nc.vector.tensor_tensor(ybias[0:C, :], banks[5][0:C, 256:257], cols[0:C, 22:23], ALU.add).then_inc(prep_cp, 1)
            for q in range(4):
                dve.wait_ge(xl[q], 16)
                with dve.Fori(0, NT // 16) as i:
                    for v in range(4):
                        nc.vector.bn_stats(st[:, q * 16 + i * 4 + v, :], x_sb[:, q * 16 + i * 4 + v, :]).then_inc(half_ready, 1)
            dve.wait_ge(half_ready, NT)
            rsqrt(EPS_C, 1)
            for k in range(TAPS):
                dve.wait_ge(prep_pe, 3 + k)
                nc.vector.tensor_copy(vlT[:, k], banks[6 + k % 2][:, 0:2 * P].rearrange("p (a b) -> p a b", a=2)).then_inc(prep_cp, 1)
            dve.wait_ge(prep_pe, 3 + TAPS)
            link(nc.vector.tensor_scalar(cv32[:, 0:8 * C], banks[0][:], WS, None, ALU.mult))
            link(nc.vector.tensor_scalar(cv32[:, 8 * C:], banks[1][:, 0:C], WS, None, ALU.mult))
            link(nc.vector.tensor_copy(cv[:, :, 0, :], cv32[:].rearrange("p (t c) -> p t c", t=TAPS)))
            link(nc.vector.tensor_tensor(cv[:, :, 1, :], cv32[:].rearrange("p (t c) -> p t c", t=TAPS), cv[:, :, 0, :], ALU.subtract))
            dve.wait_ge(ffnw, 16 * 6)
            link(nc.vector.tensor_scalar(wg_sb[:], wg_sb[:], WS, None, ALU.mult))
            link(nc.vector.tensor_copy(wg_hl[:, 0], wg_sb[:]))
            nc.vector.tensor_tensor(wg_hl[:, 1], wg_sb[:], wg_hl[:, 0], ALU.subtract).then_inc(prep_cp, 1)

            def normalise(g, src, dup, hb):
                b = g[1] % 2
                for v in range(TG):
                    o = xn[:, b, v] if dup else xn[:, b, v, 0]
                    i = src[:, idx(g, TG, v), :]
                    if dup:
                        i = i.unsqueeze(1).broadcast_to([P, 2, C])
                    ins = nc.vector.tensor_scalar(o, i, mean[:, bass.ds(idx(g, TG, v), 1)],
                                                  rstd[:, bass.ds(idx(g, TG, v), 1)], ALU.subtract, ALU.mult)
                ins.then_inc(half_ready, 1)
                wait(dve, half_ready, at(g, 2, hb + 1))
                nc.vector.tensor_copy(hl[:, b, :, 0, :], xn[:, b, :, 0, :]).then_inc(half_ready, 1)
                wait(dve, half_ready, at(g, 2, hb + 2))
                nc.vector.tensor_tensor(hl[:, b, :, 1, :], xn[:, b, :, 0, :], hl[:, b, :, 0, :],
                                        ALU.subtract).then_inc(norm_ready, 1)

            def body(g):
                nxt, prv2, nn = sh(g, 1), sh(g, -2), sh(g, 2)
                for u in range(TG):
                    t, v = tile(g, u)
                    if real(t):
                        src = dots[v % 2][:].rearrange("p (h j) -> p h j", h=HEADS)
                        wait(dve, dots_done, at(t, TG, v + 1))
                        nc.vector.tensor_reduce(mx[:, v % 2], src, axis=AX.X, op=ALU.max).then_inc(mx_ready, 1)
                        wait(dve, mx_ready, at(t, TG, v + 1))
                        wait(dve, exp_ready, at(t, TG, v - 1))
                        nc.vector.tensor_tensor(sc[:, v % 2], src, mx[:, v % 2].unsqueeze(2).broadcast_to([P, HEADS, WT]),
                                                ALU.subtract).then_inc(sub_ready, 1)
                    t, v = tile(g, u - 1)
                    if real(t):
                        wait(dve, exp_ready, at(t, TG, v + 1))
                        nc.vector.reduce_sum(sm[:, v % 2], pe_[:, v % 2], axis=AX.X).then_inc(sum_ready, 1)
                        wait(dve, sum_ready, at(t, TG, v + 1))
                        wait(dve, pn_ready, at(t, TG, v - 1))
                        nc.vector.reciprocal(rs[:, v % 2], sm[:, v % 2]).then_inc(rs_ready, 1)
                    if u == 0 and real(nxt):
                        b = nxt[1] % 2
                        src = ring[(1 + nxt[1]) % 2][:].rearrange("p (t y n c) -> p t y n c", t=TG, y=WSZ, n=2)
                        dst = bd[:, b].rearrange("p (t n) k (y c) -> p t y n k c", n=2, y=WSZ)
                        wait(dve, xt32_done, at(nxt, 1, 1))
                        wait(dve, dots_done, at(nxt, TG, -TG))
                        if is_first(nxt):
                            dve.wait_ge(zeroed, 2)
                        for k in range(2):
                            nc.vector.tensor_copy(dst[k * C:(k + 1) * C, :, :, :, k, :], src[k * C:(k + 1) * C]).then_inc(bd_ready, 1)
                    if u == 1 and real(prv2):
                        src = ring[(4 + g[1] + 1) % 2][:].rearrange("p (t k c) -> p t k c", t=TG, k=2)
                        b = prv2[1] % 2
                        wait(dve, yt_done, at(prv2, 1, 1))
                        xs = x_sb[:, bass.ds(idx(prv2, TG), TG), :]
                        xd = x1[:, bass.ds(idx(prv2, TG), TG), :]
                        nc.vector.tensor_tensor(tmp[:, b], src[:, :, 0], xs, ALU.add).then_inc(x1_ready, 1)
                        wait(dve, x1_ready, at(prv2, 2, 1))
                        nc.vector.tensor_tensor(xd, src[:, :, 1], tmp[:, b], ALU.add).then_inc(x1_ready, 1)
                        wait(dve, x1_ready, at(prv2, 2, 2))
                        for v in range(TG):
                            ins = nc.vector.bn_stats(st[:, idx(prv2, TG, v), :], x1[:, idx(prv2, TG, v), :])
                        ins.then_inc(st_ready, 1)
                    if u == 3:
                        if real(nxt):
                            for k in range(2):
                                wait(dve, bt_done, at(nxt, 2, k + 1))
                                wait(dve, z_done, at(nxt, TG, -TG))
                                nc.vector.tensor_copy(bt[:, nxt[1] % 2, k * TG:(k + 1) * TG],
                                                      ring[(7 + k + nxt[1]) % 2][:].rearrange("p (a b) -> p a b", a=TG)).then_inc(bt_ready, 1)
                        if real(nn):
                            wait(dve, xt32_done, at(nn, 1, -1))
                            normalise(nn, x_sb, True, NT)
            steps(dve, body, -2, NG + 1)

            dve.wait_ge(st_ready, NG)
            rsqrt(EPS_T, 2)

            def experts(g):
                nxt, nn, prv = sh(g, 1), sh(g, 2), sh(g, -1)

                def pair_out(t, p):
                    wait(dve, ffn2_done, at(t, CH // 2, 2 * p + 2))
                    wait(dve, wb_ready, at(t, EP, p + 1))
                    wait(dve, acc_ready, at(t, 3, (-2, -2, -1, 0)[p]))
                    nc.vector.scalar_tensor_tensor(yw[:, p], outb[p % 2][:], cols[:, 16 + p:17 + p], wb[:, t[1] % 2, p],
                                                   ALU.add, ALU.mult).then_inc(yw_ready, 1)

                halves = ring[0][:].rearrange("p (t k c) -> p t k c", t=TG, k=2)

                def residual_high():
                    wait(dve, f_done, at(prv, 1, 1))
                    nc.vector.tensor_tensor(tmp[:, prv[1] % 2], halves[:, :, 0], x1[:, bass.ds(idx(prv, TG), TG), :],
                                            ALU.add).then_inc(o_step, 1)

                def gate():
                    b = nxt[1] % 2
                    done = [0]

                    def step(ins):
                        done[0] += 1
                        ins.then_inc(gate_step, 1)

                    def after():
                        wait(dve, gate_step, at(nxt, GATE, done[0]))
                    gl = ring[1][:, 0:TG * 2 * E].rearrange("p (t k e) -> p t k e", t=TG, k=2)
                    wait(dve, gate_done, at(nxt, 1, 1))
                    step(nc.vector.scalar_tensor_tensor(lg[:, b], gl[:, :, 0], 1.0 / (XS * WS),
                                                        bg_sb[:].unsqueeze(1).broadcast_to([P, TG, E]), ALU.mult, ALU.add))
                    after()
                    step(nc.vector.scalar_tensor_tensor(lg[:, b], gl[:, :, 1], 1.0 / (XS * WS), lg[:, b], ALU.mult, ALU.add))
                    after()
                    if real(prv):
                        residual_high()
                    for v in range(TG):
                        step(nc.vector.max(top[:, b, v], lg[:, b, v]))
                    after()
                    step(nc.vector.tensor_tensor(gap[:, b], top[:, b, :, 1], top[:, b, :, 0], ALU.subtract))
                    for v in range(TG):
                        step(nc.vector.max_index(topi[:, b, v], top[:, b, v], lg[:, b, v]))
                    after()
                    step(nc.vector.tensor_copy(topf[:, b], topi[:, b, :, 0:2]))
                    after()
                    for k in range(2):
                        step(nc.vector.tensor_tensor(oh[:, b, k], iota8[:].unsqueeze(1).broadcast_to([P, TG, E]),
                                                     topf[:, b, :, k].unsqueeze(2).broadcast_to([P, TG, E]), ALU.is_equal))
                    wait(dve, tanh_ready, at(nxt, 1, 1))
                    for k in range(2):
                        step(nc.vector.tensor_scalar(w12[:, b, :, k], th[:, b], (-0.5, 0.5)[k], 0.5, ALU.mult, ALU.add))
                    after()
                    for k in range(2):
                        step(nc.vector.tensor_tensor(oh[:, b, k], oh[:, b, k],
                                                     w12[:, b, :, k].unsqueeze(2).broadcast_to([P, TG, E]), ALU.mult))
                    after()
                    step(nc.vector.tensor_tensor(wd[:, b], oh[:, b, 0], oh[:, b, 1], ALU.add))
                    after()
                    wait(dve, wt_done, at(nxt, 1, -1))
                    step(nc.vector.tensor_copy(wdh[:, b, :, 0], wd[:, b]))
                    after()
                    step(nc.vector.tensor_tensor(wdh[:, b, :, 1], wd[:, b], wdh[:, b, :, 0], ALU.subtract))
                    assert done[0] == GATE

                for j in range(CH // 2):
                    if j == 0:
                        if real(prv):
                            pair_out(prv, 3)
                        if real(nxt):
                            wait(dve, xt2_done, at(nxt, 1, 1))
                            wait(dve, h_done, at(nxt, CH, -CH))
                            nc.vector.tensor_copy(xs2[:, nxt[1] % 2], half(ring[0])).then_inc(xs2_ready, 1)
                    if j in (2, 4, 6) and real(g):
                        pair_out(g, j // 2 - 1)
                    if j == 3:
                        if real(nxt):
                            gate()
                        elif real(prv):
                            residual_high()
                        if real(prv):
                            b = prv[1] % 2
                            wait(dve, stored[b], at(sh(prv, -b), 8, 0))
                            wait(dve, o_step, at(prv, 1, 1))
                            nc.vector.tensor_tensor(ob[:, b], halves[:, :, 1], tmp[:, b], ALU.add).then_inc(out_ready, 1)
                    if j == 7 and real(nn):
                        wait(dve, xt2_done, at(nn, 1, -1))
                        normalise(nn, x1, False, NT + 2 * NG)
            steps(dve, experts, -2, NG)

        @block.tensor
        def _(pe):
            pe.wait_ge(wts, 48)
            pe.wait_ge(idn, 2)
            pe.wait_ge(wts2, 16 * 7)
            for bank, w in ((banks[0], wq_sb), (banks[1], wk_sb), (banks[2], wv_sb)):
                for h in range(HEADS):
                    nc.tensor.transpose(bank[0:DK, h * C:(h + 1) * C], w[:, h * DK:(h + 1) * DK], ident[0:C, 0:C])
            for k in range(2):
                nc.tensor.transpose(banks[3][:, k * C:(k + 1) * C], wv_sb[:, k * P:(k + 1) * P], ident[0:C, 0:C])
            nc.tensor.transpose(banks[3][:, 256:256 + 23], rows[:], ident[0:23, 0:23]).then_inc(prep_pe, 1)
            pe.wait_ge(prep_cp, 5)
            for h in range(HEADS):
                nc.tensor.matmul(banks[4][:, h * C:(h + 1) * C], wqT[:, h].rearrange("p a c -> p (a c)"), wkT[:, h],
                                 start=True, stop=True)
            for h in range(HEADS):
                o = (h % 2) * C
                nc.tensor.matmul(banks[5][o:o + C, (h // 2) * C:(h // 2 + 1) * C], wvTh[:, h], wo_h[:, h],
                                 start=True, stop=True)
            for k in range(2):
                last = nc.tensor.matmul(banks[5][0:C, 256:257], wo_sb[:, k], cols[:, 20 + k:21 + k], start=(k == 0), stop=(k == 1))
            last.then_inc(prep_pe, 1)
            pe.wait_ge(wlocs, 32)
            for k in range(TAPS):
                if k >= 2:
                    pe.wait_ge(prep_cp, 6 + k - 1)
                for oc in range(2):
                    for ic in range(2):
                        last = nc.tensor.matmul(banks[6 + k % 2][:, oc * P:(oc + 1) * P], wloc[:, ic, k, oc * P:(oc + 1) * P],
                                                wvT[:, ic].rearrange("p a c -> p (a c)"), start=(ic == 0), stop=(ic == 1))
                last.then_inc(prep_pe, 1)
            pe.wait_ge(prep_cp, 6 + TAPS)
            for k in range(TAPS):
                for oc in range(2):
                    last = nc.tensor.matmul(banks[k // 8][:, (k % 8) * C:(k % 8 + 1) * C], vlT[:, k, oc], wo_sb[:, oc],
                                            start=(oc == 0), stop=(oc == 1))
            last.then_inc(prep_pe, 1)
            pe.wait_ge(prep_cp, 7 + TAPS)

            def do_a(nxt, pr):
                k = (2, 3, 5, 6)[pr]
                b = nxt[1] % 2
                bank = ring[(k + nxt[1]) % 2]
                rhs = xsp[:, b, :, 1:1 + HI, 1:1 + WI]
                for hv, wsp in enumerate((g_hi, g_lo)):
                    last = nc.tensor.matmul(bank[:], wsp[:, pr * P:(pr + 1) * P], rhs, start=(hv == 0), stop=(hv == 1))
                last.then_inc(a_done, 1)

            def body(g):
                nxt, prv, prv2 = sh(g, 1), sh(g, -1), sh(g, -2)
                for u in range(TG):
                    t, v = tile(g, u)
                    if real(t):
                        b = t[1] % 2
                        if v == 0:
                            wait(pe, a_ready, at(t, PAIRS, PAIRS))
                            wait(pe, bd_ready, at(t, 2, 2))
                        wait(pe, sub_ready, at(t, TG, v - 1))
                        for pr in range(PAIRS):
                            for w in range(2):
                                last = nc.tensor.matmul(
                                    dots[v % 2][w * WT:(w + 1) * WT, pr * P:(pr + 1) * P],
                                    aa[:, b, pr, w * TG * WT + v * WT:w * TG * WT + (v + 1) * WT],
                                    bd[:, b, 2 * v + w].rearrange("p a j -> p (a j)"), start=True, stop=True)
                        last.then_inc(dots_done, 1)
                    b1_ = nxt[1] % 2
                    if u == 0 and real(nxt):
                        wait(pe, norm_ready, at(nxt, 1, 1))
                        wait(pe, bt_ready, at(nxt, 2, -1))
                        for k in range(TG):
                            last = nc.tensor.transpose(half(ring[b1_])[:, k * P:(k + 1) * P],
                                                       hl[:, b1_, k].rearrange("p a c -> p (a c)"), ident16[:])
                        last.then_inc(x16_done, 1)
                        wait(pe, bt_ready, at(nxt, 2, 0))
                        for k in range(TG):
                            last = nc.tensor.transpose(ring[(1 + b1_) % 2][:, k * P:(k + 1) * P],
                                                       xn[:, b1_, k].rearrange("p a c -> p (a c)"), ident[:])
                        last.then_inc(xt32_done, 1)
                    if u == 1:
                        if real(nxt):
                            wait(pe, xsp_ready, at(nxt, 1, 1))
                            do_a(nxt, 0)
                            wait(pe, bd_ready, at(nxt, 2, 2))
                            do_a(nxt, 1)
                        if real(prv2):
                            if real(nxt):
                                wait(pe, a_ready, at(nxt, PAIRS, 1))
                            else:
                                wait(pe, bt_ready, 2 * NG)
                                wait(pe, x1_ready, at(prv2, 2, -2))
                            wait(pe, y_ready, at(prv2, 1, 1))
                            bank = ring[(4 + g[1] + 1) % 2]
                            for k in range(TG):
                                last = nc.tensor.transpose(bank[:, k * P:(k + 1) * P], ys[:, prv2[1] % 2, k * P:(k + 1) * P], ident[:])
                            last.then_inc(yt_done, 1)
                    if u == 2:
                        if real(nxt):
                            wait(pe, a_ready, at(nxt, PAIRS, 2))
                            do_a(nxt, 2)
                            wait(pe, a_ready, at(nxt, PAIRS, 1))
                            if real(prv2):
                                wait(pe, x1_ready, at(prv2, 2, 2))
                            do_a(nxt, 3)
                        if real(g):
                            wait(pe, y_ready, at(g, 1, -1))
                            for k in range(TAPS):
                                rhs = xsp[:, g[1] % 2, :, k // 3:k // 3 + HI, k % 3:k % 3 + WI]
                                last = nc.tensor.matmul(outb[g[1] % 2][:], cv[:, k].rearrange("p a c -> p (a c)"), rhs,
                                                        start=(k == 0), stop=False, skip_group_check=True)
                            last.then_inc(conv_done, 1)
                    if u == 3:
                        if real(nxt):
                            for k in range(2):
                                wait(pe, a_ready, at(nxt, PAIRS, 3 + k))
                                for a in range(TG):
                                    last = nc.tensor.transpose(ring[(7 + k + b1_) % 2][:, a * P:(a + 1) * P],
                                                               bd[:, b1_, k * TG + a].rearrange("p a j -> p (a j)"), ident[:])
                                last.then_inc(bt_done, 1)
                        if real(prv):
                            wait(pe, z_ready, at(prv, TG, TG))
                            for k in range(2):
                                for hf in range(2):
                                    pr = 2 * hf + k
                                    rhs = zs[:, prv[1] % 2, :, pr, :]
                                    last = nc.tensor.matmul(outb[prv[1] % 2][hf * C:(hf + 1) * C, :], wvo[:, pr], rhs,
                                                            start=False, stop=(k == 1), skip_group_check=True)
                            last.then_inc(att_done, 1)
                    t, v = tile(g, u - 2)
                    if real(t):
                        wait(pe, pn_ready, at(t, TG, v + 1))
                        wait(pe, pt_ready, at(t, TG, v))
                        for pr in range(PAIRS):
                            last = nc.tensor.transpose(ptb[:, pr * P:(pr + 1) * P], pn[:, v % 2, pr * P:(pr + 1) * P], ident[:])
                        last.then_inc(pt_done, 1)
                    t, v = tile(g, u - 3)
                    if real(t):
                        wait(pe, pt_ready, at(t, TG, v + 1))
                        wait(pe, bt_ready, at(t, 2, 2))
                        wait(pe, z_ready, at(t, TG, v))
                        zo = zb[:].rearrange("p (a y n c) -> p a y n c", a=PAIRS, y=WSZ, n=2)
                        for w in range(2):
                            last = nc.tensor.matmul(zo[:, :, :, w, :], bt[:, t[1] % 2, 2 * v + w],
                                                    pt[:, v % 2, :, w * WT:(w + 1) * WT], start=True, stop=True)
                        last.then_inc(z_done, 1)
            steps(pe, body, -1, NG + 1)

            pe.wait_ge(w1_ready, 3)

            def experts(g):
                nxt, prv = sh(g, 1), sh(g, -1)

                def ffn2(t, j):
                    for c in (2 * j, 2 * j + 1):
                        e, k = expert(c)
                        hf = (e % 2) * C
                        wait(pe, gelu_ready, at(t, CH, c + 1))
                        if k == 0 and c % 2 == 0:
                            wait(pe, yw_ready, at(t, EP, c // 4 - 1))
                        last = nc.tensor.matmul(outb[(c // 4) % 2][hf:hf + C, :], w2_sb[:, e, k], hh[:, c % 4],
                                                start=(k == 0), stop=(k == 1))
                    last.then_inc(ffn2_done, 1)

                for j in range(CH // 2):
                    if real(g):
                        for c in (2 * j, 2 * j + 1):
                            e, k = expert(c)
                            if c == 0:
                                wait(pe, xs2_ready, at(g, 1, 1))
                            wait(pe, gelu_ready, at(g, CH, c - 3))
                            o = (2 * e + k) * P
                            nc.tensor.matmul(hidb[c % 4][:], w1_hi[:, o:o + P], xs2[:, g[1] % 2], start=True, stop=False)
                            nc.tensor.matmul(hidb[c % 4][:], w1_lo[:, o:o + P], xs2[:, g[1] % 2], start=False,
                                             stop=True).then_inc(h_done, 1)
                    if j == 0 and real(prv):
                        ffn2(prv, CH // 2 - 1)
                    if j > 0 and real(g):
                        ffn2(g, j - 1)
                    if j == 0 and real(nxt):
                        wait(pe, norm_ready, at(nxt, 1, NG + 1))
                        wait(pe, wb_ready, at(nxt, EP, -1))
                        for k in range(TG):
                            last = nc.tensor.transpose(half(ring[0])[:, k * P:(k + 1) * P],
                                                       hl[:, nxt[1] % 2, k].rearrange("p a c -> p (a c)"), ident16[:])
                        last.then_inc(xt2_done, 1)
                    if j == 1 and real(nxt):
                        wait(pe, xs2_ready, at(nxt, 1, 1))
                        wait(pe, wb_ready, at(nxt, EP, 0))
                        for v in range(TG):
                            last = nc.tensor.matmul(ring[1][:, v * 2 * E:(v + 1) * 2 * E], xs2[:, nxt[1] % 2, v * P:(v + 1) * P],
                                                    wg_hl[:].rearrange("p k e -> p (k e)"), start=True, stop=True)
                        last.then_inc(gate_done, 1)
                    if j == 3 and real(prv):
                        wait(pe, acc_ready, at(prv, 3, 3))
                        if not real(nxt):
                            wait(pe, out_ready, at(prv, 1, 0))
                            wait(pe, wb_ready, EP * NG)
                        for k in range(TG):
                            last = nc.tensor.transpose(ring[0][:, k * P:(k + 1) * P], acc[:, prv[1] % 2, k * P:(k + 1) * P], ident[:])
                        last.then_inc(f_done, 1)
                    if j == 5 and real(nxt):
                        wait(pe, gate_step, at(nxt, GATE, GATE))
                        for k in range(TG):
                            last = nc.tensor.transpose(half(ring[1])[0:2 * E, k * P:(k + 1) * P],
                                                       wdh[:, nxt[1] % 2, k].rearrange("p a e -> p (a e)"), ident16[:])
                        last.then_inc(wt_done, 1)
                    if j in (6, 7) and real(nxt):
                        for p in (2 * (j - 6), 2 * (j - 6) + 1):
                            wait(pe, wt_ready, at(nxt, 1, 1))
                            if p == 0:
                                wait(pe, out_ready, at(prv, 1, 1))
                            wait(pe, wb_ready, at(nxt, EP, p - 1))
                            nc.tensor.matmul(ring[p % 2][:], sel[:, p], wdT[:, nxt[1] % 2], start=True,
                                             stop=True).then_inc(wb_done, 1)
            steps(pe, experts, -1, NG)


_INS = ['x', 'L0_conv_w_q', 'L0_conv_w_k', 'L0_conv_w_v', 'L0_conv_w_local', 'L0_conv_b_local', 'L0_conv_w_out',
        'L0_conv_b_out', 'L0_ffn_Wg', 'L0_ffn_bg', 'L0_ffn_W1', 'L0_ffn_b1', 'L0_ffn_W2', 'L0_ffn_b2']


def kernel(**inputs):
    import concourse.bacc as bacc
    from concourse.bass_utils import run_bass_kernel_spmd

    nc = bacc.Bacc("TRN2", target_bir_lowering=False, num_devices=1)
    arrays, args = {}, []
    for name in _INS:
        a = np.ascontiguousarray(inputs[name])
        if name == 'x':
            a = a.reshape(B * HI * WI, C)
        arrays[f"in_{name}"] = a
        args.append(nc.dram_tensor(f"in_{name}", a.shape, mybir.dt.from_np(a.dtype), kind="ExternalInput").ap())
    args.append(nc.dram_tensor("out", (B * HI * WI, C), F32, kind="ExternalOutput").ap())
    program(nc, *args)
    r = run_bass_kernel_spmd(nc, [arrays], core_ids=[0])
    return r.results[0]["out"].reshape(B, HI, WI, C)
```

```python
import numpy as np

import concourse.bass as bass
from concourse import mybir
from contextlib import ExitStack

F32 = mybir.dt.float32
F16 = mybir.dt.float16
U32 = mybir.dt.uint32
ACT = mybir.ActivationFunctionType
ALU = mybir.AluOpType
AX = mybir.AxisListType

B, HI, WI, C = 32, 16, 16, 64
HEADS, DK, WSZ = 8, 32, 8
HC = HEADS * DK
E, HID = 8, 256
P = 128
WT = WSZ * WSZ
NT = B * HI * WI // P
TG = 4
NG = NT // TG
GT = TG * P
IG = GT // (HI * WI)
PAIRS = HEADS // 2
EP = E // 2
TAPS = 9
PADW = WI + 2
CH = E * HID // P
EPS_C, EPS_T = 1e-6, 1e-5
SCALE = DK ** -0.5
XS = 16.0
WS = 16.0


def at(g, per, extra):
    i, off = g
    static = off * per + extra
    return static if i is None else i * (2 * per) + static


def sh(g, d):
    return (g[0], g[1] + d)


def real(g):
    return g[0] is not None or 0 <= g[1] < NG


def is_step(g, s):
    return g[0] is None and g[1] == s


def tile(g, u):
    return sh(g, u // TG), u % TG


def idx(g, per, extra=0):
    return at(g, per, extra)


def wait(eng, sem, value):
    if isinstance(value, int) and value <= 0:
        return
    eng.wait_ge(sem, value)


def steps(eng, body, first, last):
    for s in range(first, 4):
        body((None, s))
    with eng.Fori(2, NG // 2 - 1) as i:
        body((i, 0))
        body((i, 1))
    for s in range(NG - 2, last + 1):
        body((None, s))


def expert(c):
    return 2 * (c // 4) + c % 2, (c % 4) // 2


N2 = NT - 4 * TG
TP = (TAPS + 1) // 2
QT = NT // 4
GATE = 21


def program(nc, x, w_q, w_k, w_v, w_local, b_local, w_out, b_out, wg, bg, w1, b1, w2, b2, out):
    ctx = ExitStack()
    with ctx:
        def sb(name, shape, dt=F32):
            return ctx.enter_context(nc.sbuf_tensor(name, shape, dt))

        def sem(name):
            return ctx.enter_context(nc.semaphore(name))

        ident = sb("ident", [P, P])
        ident16 = sb("ident16", [P, P], F16)
        iota8 = sb("iota8", [P, E])
        sel = sb("sel", [2 * E, EP, P], F16)
        wq_sb = sb("wq_sb", [C, HC])
        wk_sb = sb("wk_sb", [C, HC])
        wv_sb = sb("wv_sb", [C, HC])
        wqT = sb("wqT", [DK, HEADS, 2, C])
        wkT = sb("wkT", [DK, HEADS, C])
        wvTh = sb("wvTh", [DK, HEADS, C])
        wvT = sb("wvT", [P, 2, C])
        wloc = sb("wloc", [P, 2, TAPS, HC])
        wo_sb = sb("wo_sb", [P, 2, C])
        wo_h = sb("wo_h", [DK, HEADS, C])
        vl = sb("vl", [P, TP, HC])
        vlT = sb("vlT", [P, TP, 2, P])
        rows = sb("rows", [23, P])
        cols = sb("cols", [P, 23])
        ybias = sb("ybias", [P, 1])
        bg_sb = sb("bg_sb", [P, E])
        g32 = sb("g32", [P, HEADS * C])
        g_hi = sb("g_hi", [P, HEADS * C], F16)
        g_lo = sb("g_lo", [P, HEADS * C], F16)
        cv32 = sb("cv32", [C, TAPS * C])
        cv = sb("cv", [P, TAPS, 2, C], F16)
        wvo = sb("wvo", [P, PAIRS, C])
        w1_sb = sb("w1_sb", [P, E * HID])
        w1_hi = sb("w1_hi", [P, E * HID], F16)
        w1_lo = sb("w1_lo", [P, E * HID], F16)
        wg_sb = sb("wg_sb", [P, E])
        wg_hl = sb("wg_hl", [P, 2, E], F16)
        w2_sb = sb("w2_sb", [P, E, 2, C])
        x_sb = sb("x_sb", [P, NT, C])
        x1 = sb("x1", [P, NT, C])
        st = sb("st", [P, NT, 6])
        mean = sb("mean", [P, NT])
        rstd = sb("rstd", [P, NT])
        va = sb("va", [P, NT])
        vb = sb("vb", [P, NT])
        vc = sb("vc", [P, NT])
        xn = sb("xn", [P, 2, TG, 2, C])
        hl = sb("hl", [P, 2, TG, 2, C], F16)
        xsp = sb("xsp", [P, 2, IG, PADW, PADW], F16)
        bd = sb("bd", [P, 2, TG * 2, 2, WT])
        bt = sb("bt", [P, 2, TG * 2, P])
        aa = sb("aa", [P, 2, PAIRS, GT])
        sc = sb("sc", [P, 2, HEADS, WT])
        pe_ = sb("pe_", [P, 2, HEADS, WT])
        pn = sb("pn", [P, 2, HEADS * WT])
        pt = sb("pt", [P, 2, PAIRS, P])
        mx = sb("mx", [P, 2, HEADS])
        sm = sb("sm", [P, 2, HEADS])
        rs = sb("rs", [P, 2, HEADS])
        zs = sb("zs", [P, 2, TG, PAIRS, P])
        ys = sb("ys", [P, 2, GT])
        tmp = sb("tmp", [P, 2, TG, C])
        xs2 = sb("xs2", [P, 2, GT], F16)
        lg = sb("lg", [P, 2, TG, E])
        top = sb("top", [P, 2, TG, 8])
        topi = sb("topi", [P, 2, TG, 8], U32)
        topf = sb("topf", [P, 2, TG, 2])
        gap = sb("gap", [P, 2, TG])
        th = sb("th", [P, 2, TG])
        w12 = sb("w12", [P, 2, TG, 2])
        oh = sb("oh", [P, 2, 2, TG, E])
        wd = sb("wd", [P, 2, TG, E])
        wdh = sb("wdh", [P, 2, TG, 2, E], F16)
        wdT = sb("wdT", [2 * E, 2, GT], F16)
        wb = zs[:].rearrange("p b t a c -> p b t (a c)")
        wl = wloc[:].rearrange("p k t o -> p k (t o)")
        hh = wl[:, 0, 0:4 * GT].rearrange("p (a b) -> p a b", a=4)
        yw = wl[:, 1, 0:EP * GT].rearrange("p (a b) -> p a b", a=EP)
        acc = sb("acc", [P, 2, GT])
        ob = sb("ob", [P, 2, TG, C])

        banks = [ctx.enter_context(nc.psum_tensor(f"bank{i}", [P, 512], F32)) for i in range(8)]

        wqkv_in = sem("wqkv_in")
        wout_in = sem("wout_in")
        wlocs = sem("wlocs")
        rows_in = sem("rows_in")
        ffnw = sem("ffnw")
        xl = [sem(f"xl{i}") for i in range(4)]
        idn = sem("idn")
        wT_done = sem("wT_done")
        qk_ready = sem("qk_ready")
        v_ready = sem("v_ready")
        g_done = sem("g_done")
        g_ready = sem("g_ready")
        wvo_done = sem("wvo_done")
        wvo_ready = sem("wvo_ready")
        vl_done = sem("vl_done")
        vl_ready = sem("vl_ready")
        cols_done = sem("cols_done")
        cols_ready = sem("cols_ready")
        vlT_done = sem("vlT_done")
        vlT_ready = sem("vlT_ready")
        cw_done = sem("cw_done")
        cw_ready = sem("cw_ready")
        ybias_ready = sem("ybias_ready")
        cv_ready = sem("cv_ready")
        cv_in = sem("cv_in")
        gatew_ready = sem("gatew_ready")
        dself = sem("dself")
        pself = sem("pself")
        w1_ready = sem("w1_ready")
        sq_in = sem("sq_in")
        sq_done = sem("sq_done")
        zeroed = sem("zeroed")
        norm_ready = sem("norm_ready")
        x16_done = sem("x16_done")
        xt32_done = sem("xt32_done")
        xsp_ready = sem("xsp_ready")
        bd_ready = sem("bd_ready")
        a_done = sem("a_done")
        a_ready = sem("a_ready")
        bt_done = sem("bt_done")
        bt_ready = sem("bt_ready")
        dots_done = sem("dots_done")
        mx_ready = sem("mx_ready")
        sub_ready = sem("sub_ready")
        exp_ready = sem("exp_ready")
        sum_ready = sem("sum_ready")
        rs_ready = sem("rs_ready")
        pn_ready = sem("pn_ready")
        pt_done = sem("pt_done")
        pt_ready = sem("pt_ready")
        z_done = sem("z_done")
        z_ready = sem("z_ready")
        conv_done = sem("conv_done")
        att_done = sem("att_done")
        y_ready = sem("y_ready")
        yt_done = sem("yt_done")
        x1_ready = sem("x1_ready")
        half_ready = sem("half_ready")
        st_ready = sem("st_ready")
        xt2_done = sem("xt2_done")
        xs2_ready = sem("xs2_ready")
        gate_done = sem("gate_done")
        gate_step = sem("gate_step")
        tanh_ready = sem("tanh_ready")
        wt_done = sem("wt_done")
        wt_ready = sem("wt_ready")
        wb_done = sem("wb_done")
        wb_ready = sem("wb_ready")
        h_done = sem("h_done")
        gelu_ready = sem("gelu_ready")
        ffn2_done = sem("ffn2_done")
        yw_ready = sem("yw_ready")
        acc_ready = sem("acc_ready")
        f_done = sem("f_done")
        o_step = sem("o_step")
        out_ready = sem("out_ready")
        stored = [sem(f"stored{i}") for i in range(2)]

        block = ctx.enter_context(nc.Block())

        x_tiles = x.rearrange("(t p) d -> p t d", p=P)
        out_tiles = out.rearrange("(t p) d -> p t d", p=P)

        dots = [banks[0], banks[1]]
        ptb, zb = banks[2], banks[3]
        attb = banks[4]
        BTA, BTB, X16, XT32, A0, A1, YT, A2, A3 = range(9)
        turn = [banks[5 + k % 3] for k in range(9)]
        a_turn = (A0, A1, A2, A3)
        hidb = [banks[i] for i in range(4)]
        outb = [banks[4], banks[5]]
        ring = [banks[6], banks[7]]

        vltb = [banks[0], banks[2], banks[3]]

        def half(bank):
            return bank[:, 0:256].bitcast(F16)

        @block.sync
        def _(sp):
            sp.dma_start(wq_sb[:], w_q[0, 0]).then_inc(wqkv_in, 16)
            sp.dma_start(wk_sb[:], w_k[0, 0]).then_inc(wqkv_in, 16)
            sp.dma_start(wv_sb[:], w_v[0, 0]).then_inc(wqkv_in, 16)
            sp.dma_start(x_sb[:, 0:QT, :], x_tiles[:, 0:QT, :]).then_inc(xl[0], 16)
            for k in range(2):
                sp.dma_start(wloc[:, k], w_local.rearrange("a b i o -> i (a b) o")[k * P:(k + 1) * P]).then_inc(wlocs, 16)
            sp.dma_start(rows[0:16, :], b1.rearrange("e (k n) -> (e k) n", n=P)).then_inc(rows_in, 16)
            sp.dma_start(rows[16:20, :], b2.rearrange("(p e) n -> p (e n)", e=2)).then_inc(rows_in, 16)
            sp.dma_start(rows[20:22, :], b_local.rearrange("(k n) -> k n", n=P)).then_inc(rows_in, 16)
            for k in range(2):
                sp.dma_start(rows[22:23, k * C:(k + 1) * C], b_out.unsqueeze(0)).then_inc(rows_in, 16)
            for q in range(1, 4):
                sp.dma_start(x_sb[:, q * QT:(q + 1) * QT, :], x_tiles[:, q * QT:(q + 1) * QT, :]).then_inc(xl[q], 16)
            sp.dma_start(bg_sb[:], bg.unsqueeze(0).broadcast_to([P, E])).then_inc(ffnw, 16)
            for h in range(2):
                sp.dma_start(wg_sb[h * C:(h + 1) * C, :], wg).then_inc(ffnw, 16)
            for h in range(2):
                sp.dma_start(w1_sb[h * C:(h + 1) * C, :].rearrange("c (e n) -> c e n", e=E),
                             w1.rearrange("e c n -> c e n")).then_inc(ffnw, 16)
            sp.dma_start(w2_sb[:], w2.rearrange("e (k n) c -> n e k c", n=P)).then_inc(ffnw, 16)

            sp.wait_ge(cv_ready, 2)
            sp.dma_start(cv[C:P], cv[0:C]).then_inc(cv_in, 16)

            def body(g):
                prv = sh(g, -1)
                if real(prv):
                    b = prv[1] % 2
                    wait(sp, out_ready, at(prv, 1, 1))
                    sp.dma_start(out_tiles[:, bass.ds(idx(prv, TG), TG), :], ob[:, b]).then_inc(stored[b], 16)
            steps(sp, body, 0, NG)
            for b in range(2):
                sp.wait_ge(stored[b], 16 * (NG // 2))

        @block.gpsimd
        def _(pool):
            nc.gpsimd.memset(ident[:], 0.0).then_inc(pself, 1)
            nc.gpsimd.iota(iota8[:], [[1, E]], base=0, channel_multiplier=0,
                           allow_small_or_imprecise_dtypes=True).then_inc(idn, 1)
            pool.wait_ge(pself, 1)
            nc.gpsimd.affine_select(out=ident[:], in_=ident[:], compare_op=ALU.not_equal, fill=1.0, base=0,
                                    pattern=[[-1, P]], channel_multiplier=1).then_inc(idn, 1)
            pool.wait_ge(idn, 2)
            nc.gpsimd.tensor_copy(ident16[:], ident[:]).then_inc(idn, 1)
            nc.gpsimd.memset(xsp[:], 0.0).then_inc(zeroed, 1)
            nc.gpsimd.memset(bd[:], 0.0).then_inc(zeroed, 1)

            def body(g):
                if is_step(g, 2):
                    pool.wait_ge(w1_ready, 2)
                    nc.gpsimd.tensor_tensor(w1_lo[:], w1_sb[:], w1_hi[:], ALU.subtract).then_inc(w1_ready, 1)
                for u in range(TG):
                    t, v = tile(g, u)
                    if not real(t):
                        continue
                    wait(pool, rs_ready, at(t, TG, v + 1))
                    wait(pool, pt_done, at(t, TG, v - 1))
                    nc.gpsimd.tensor_tensor(pn[:, v % 2, :].rearrange("p (h j) -> p h j", h=HEADS), pe_[:, v % 2],
                                            rs[:, v % 2].unsqueeze(2).broadcast_to([P, HEADS, WT]),
                                            ALU.mult).then_inc(pn_ready, 1)
            steps(pool, body, 0, NG - 1)

            def experts(g):
                if not real(g):
                    return
                b = g[1] % 2
                wait(pool, f_done, at(g, 1, -1))
                wait(pool, yw_ready, at(g, EP, 2))
                nc.gpsimd.tensor_tensor(acc[:, b], yw[:, 0], yw[:, 1], ALU.add).then_inc(acc_ready, 1)
                for p in (2, 3):
                    wait(pool, yw_ready, at(g, EP, p + 1))
                    wait(pool, acc_ready, at(g, 3, p - 1))
                    nc.gpsimd.tensor_tensor(acc[:, b], acc[:, b], yw[:, p], ALU.add).then_inc(acc_ready, 1)
            steps(pool, experts, 0, NG - 1)

        @block.scalar
        def _(act):
            act.dma_start(wo_h[:], w_out[0, 0].rearrange("(h d) o -> d h o", d=DK)).then_inc(wout_in, 16)
            act.dma_start(wo_sb[:], w_out[0, 0].rearrange("(k i) o -> i k o", i=P)).then_inc(wout_in, 16)

            act.wait_ge(wT_done, 1)
            nc.scalar.copy(wkT[:], banks[1][0:DK, :].rearrange("p (h c) -> p h c", h=HEADS)).then_inc(qk_ready, 1)
            act.wait_ge(wT_done, 2)
            nc.scalar.copy(wvTh[:], banks[2][0:DK, :].rearrange("p (h c) -> p h c", h=HEADS)).then_inc(v_ready, 1)
            nc.scalar.copy(wvT[:], banks[3][:, 0:2 * C].rearrange("p (k c) -> p k c", k=2)).then_inc(v_ready, 1)
            act.wait_ge(sq_in, 1)
            nc.scalar.sqrt(vb[:, 0:QT], va[:, 0:QT]).then_inc(sq_done, 1)

            def gate_tanh(t):
                wait(act, gate_step, at(t, GATE, 7))
                nc.scalar.activation(th[:, t[1] % 2], gap[:, t[1] % 2], ACT.Tanh, scale=0.5).then_inc(tanh_ready, 1)

            def weights_out(t):
                wait(act, wt_done, at(t, 1, 1))
                wait(act, wb_done, at(t, EP, -EP))
                nc.scalar.copy(wdT[:, t[1] % 2], half(ring[1])[0:2 * E]).then_inc(wt_ready, 1)

            def spread_out(t, p):
                wait(act, wb_done, at(t, EP, p + 1))
                wait(act, yw_ready, at(t, EP, -EP))
                nc.scalar.copy(wb[:, t[1] % 2, p], ring[p % 2][:]).then_inc(wb_ready, 1)

            first = (None, 0)

            def body(g):
                nxt = sh(g, 1)
                if is_step(g, 0):
                    for j in range(2):
                        act.wait_ge(vl_done, j + 1)
                        nc.scalar.copy(vl[:, 2 * j:2 * j + 2], banks[2 + j][:].rearrange("p (m o) -> p m o", m=2)).then_inc(vl_ready, 1)
                    act.wait_ge(vl_done, 3)
                    nc.scalar.copy(vl[0:C, TP - 1], banks[4][0:C, 0:HC]).then_inc(vl_ready, 1)
                    for j in range(2):
                        act.wait_ge(vlT_done, j + 1)
                        nc.scalar.copy(vlT[:, 2 * j:2 * j + 2], vltb[j][:].rearrange("p (m a c) -> p m a c", m=2, a=2)).then_inc(vlT_ready, 1)
                    act.wait_ge(vlT_done, 3)
                    nc.scalar.copy(vlT[:, TP - 1, :, 0:C], vltb[2][:, 0:2 * C].rearrange("p (a c) -> p a c", a=2)).then_inc(vlT_ready, 1)
                    act.wait_ge(cw_done, 1)
                    nc.scalar.mul(cv32[:, 0:8 * C], banks[4][0:C, :], WS).then_inc(cw_ready, 1)
                    act.wait_ge(cw_done, 2)
                    nc.scalar.mul(cv32[:, 8 * C:], banks[3][0:C, 0:C], WS).then_inc(cw_ready, 1)
                if is_step(g, 2):
                    act.wait_ge(sq_in, 2)
                    nc.scalar.sqrt(vb[:, QT:], va[:, QT:]).then_inc(sq_done, 1)
                if is_step(g, 2):
                    act.wait_ge(ffnw, 16 * 6)
                    nc.scalar.mul(w1_sb[:], w1_sb[:], WS).then_inc(w1_ready, 1)
                    act.wait_ge(w1_ready, 1)
                    nc.scalar.copy(w1_hi[:], w1_sb[:]).then_inc(w1_ready, 1)
                if is_step(g, NG - 1):
                    act.wait_ge(sq_in, 3)
                    nc.scalar.sqrt(vb[:, 0:N2], va[:, 0:N2]).then_inc(sq_done, 1)
                for u in range(TG):
                    if real(nxt):
                        if u == 1:
                            wait(act, x16_done, at(nxt, 1, 1))
                            wait(act, conv_done, at(nxt, 1, -1))
                            if is_step(nxt, 0):
                                act.wait_ge(zeroed, 1)
                            b = nxt[1] % 2
                            src = half(turn[X16])
                            nc.scalar.copy(xsp[:, b, :, 1:1 + HI, 1:1 + WI],
                                           src.rearrange("p (m y c) -> p m y c", m=IG, y=HI)).then_inc(xsp_ready, 1)
                        if u in (2, 3):
                            for pr in (2 * (u - 2), 2 * (u - 2) + 1):
                                wait(act, a_done, at(nxt, PAIRS, pr + 1))
                                wait(act, dots_done, at(nxt, TG, -TG))
                                src = turn[a_turn[pr]]
                                dst = aa[:, nxt[1] % 2, pr, :].rearrange("p (n ty c) -> p ty n c", n=2, c=WSZ)
                                nc.scalar.mul(dst, src[:].rearrange("p (ty n c) -> p ty n c", n=2, c=WSZ),
                                              1.0 / WS).then_inc(a_ready, 1)
                    t, v = tile(g, u)
                    if real(t):
                        wait(act, sub_ready, at(t, TG, v + 1))
                        wait(act, pn_ready, at(t, TG, v - 1))
                        wait(act, sum_ready, at(t, TG, v - 1))
                        nc.scalar.activation(pe_[:, v % 2], sc[:, v % 2], ACT.Exp,
                                             scale=SCALE / XS / XS).then_inc(exp_ready, 1)
                    t, v = tile(g, u - 2)
                    if real(t):
                        wait(act, pt_done, at(t, TG, v + 1))
                        wait(act, z_done, at(t, TG, v - 1))
                        nc.scalar.copy(pt[:, v % 2], ptb[:].rearrange("p (a b) -> p a b", a=PAIRS)).then_inc(pt_ready, 1)
                    t, v = tile(g, u - 3)
                    if real(t):
                        wait(act, z_done, at(t, TG, v + 1))
                        wait(act, att_done, at(t, 1, -1))
                        nc.scalar.copy(zs[:, t[1] % 2, v], zb[:].rearrange("p (a b) -> p a b", a=PAIRS)).then_inc(z_ready, 1)
                    if is_step(g, NG) and u == 2:
                        gate_tanh(first)
                    if is_step(g, NG) and u == 3:
                        weights_out(first)
                    prv = sh(g, -1)
                    if u == TG - 1 and real(prv):
                        wait(act, att_done, at(prv, 1, 1))
                        wait(act, yt_done, at(prv, 1, -1))
                        nc.scalar.activation(ys[:, prv[1] % 2, :], attb[:], ACT.Identity, scale=1.0 / (XS * WS), bias=ybias[:, 0:1]).then_inc(y_ready, 1)
                if is_step(g, NG):
                    for p in range(EP):
                        spread_out(first, p)
            steps(act, body, -1, NG)

            def experts(g):
                nxt = sh(g, 1)
                if is_step(g, 1):
                    act.wait_ge(sq_in, 4)
                    nc.scalar.sqrt(vb[:, N2:], va[:, N2:]).then_inc(sq_done, 1)
                for j in range(CH // 2):
                    if real(g):
                        for c in (2 * j, 2 * j + 1):
                            e, k = expert(c)
                            wait(act, h_done, at(g, CH, c + 1))
                            wait(act, ffn2_done, at(g, CH // 2, (c - 4) // 2 + 1))
                            nc.scalar.activation(hh[:, c % 4], hidb[c % 4][:], ACT.Gelu, scale=1.0 / (XS * WS),
                                                 bias=cols[:, 2 * e + k:2 * e + k + 1]).then_inc(gelu_ready, 1)
                    if j == 3 and real(nxt):
                        gate_tanh(nxt)
                    if j == 5 and real(nxt):
                        weights_out(nxt)
                    if j in (6, 7) and real(nxt):
                        spread_out(nxt, 2 * (j - 6))
                        spread_out(nxt, 2 * (j - 6) + 1)
            steps(act, experts, 0, NG - 1)

        @block.vector
        def _(dve):
            n = [0]

            def link(ins):
                n[0] += 1
                ins.then_inc(dself, 1)
                dve.wait_ge(dself, n[0])

            def rsqrt(eps, count, lo, hi, between=None):
                me, qe, mo, qo = (st[:, lo:hi, k] for k in (1, 2, 4, 5))
                m, r, a, b_, v = (t[:, lo:hi] for t in (mean, rstd, va, vb, vc))
                link(nc.vector.tensor_tensor(m, me, mo, ALU.add))
                link(nc.vector.tensor_tensor(a, me, mo, ALU.subtract))
                link(nc.vector.tensor_tensor(b_, qe, qo, ALU.add))
                link(nc.vector.tensor_scalar(m, m, 0.5, None, ALU.mult))
                link(nc.vector.tensor_tensor(a, a, a, ALU.mult))
                link(nc.vector.tensor_scalar(b_, b_, 1.0 / C, eps, ALU.mult, ALU.add))
                link(nc.vector.scalar_tensor_tensor(v, a, 0.25, b_, ALU.mult, ALU.add))
                nc.vector.tensor_copy(a, v).then_inc(sq_in, 1)
                if between:
                    between()
                dve.wait_ge(sq_done, count)
                link(nc.vector.reciprocal(r, b_))
                link(nc.vector.tensor_tensor(b_, r, r, ALU.mult))
                link(nc.vector.tensor_tensor(a, b_, v, ALU.mult))
                link(nc.vector.tensor_scalar(a, a, -0.5 * XS, 1.5 * XS, ALU.mult, ALU.add))
                link(nc.vector.tensor_tensor(r, r, a, ALU.mult))

            def statistics(q):
                dve.wait_ge(xl[q], 16)
                for v in range(q * QT, (q + 1) * QT):
                    nc.vector.bn_stats(st[:, v, :], x_sb[:, v, :]).then_inc(half_ready, 1)

            def split_g():
                dve.wait_ge(g_done, 1)
                link(nc.vector.tensor_scalar(g32[:], banks[4][:], WS, None, ALU.mult))
                link(nc.vector.tensor_copy(g_hi[:], g32[:]))
                nc.vector.tensor_tensor(g_lo[:], g32[:], g_hi[:], ALU.subtract).then_inc(g_ready, 1)

            dve.wait_ge(wT_done, 1)
            nc.vector.tensor_copy(wqT[:], banks[0][0:DK, :].rearrange("p (h c) -> p h c", h=HEADS)
                                  .unsqueeze(2).broadcast_to([DK, HEADS, 2, C])).then_inc(qk_ready, 1)
            statistics(0)
            dve.wait_ge(half_ready, QT)
            rsqrt(EPS_C, 1, 0, QT, split_g)

            def normalise(g, src, dup, hb):
                b = g[1] % 2
                for v in range(TG):
                    o = xn[:, b, v] if dup else xn[:, b, v, 0]
                    i = src[:, idx(g, TG, v), :]
                    if dup:
                        i = i.unsqueeze(1).broadcast_to([P, 2, C])
                    ins = nc.vector.tensor_scalar(o, i, mean[:, bass.ds(idx(g, TG, v), 1)],
                                                  rstd[:, bass.ds(idx(g, TG, v), 1)], ALU.subtract, ALU.mult)
                ins.then_inc(half_ready, 1)
                wait(dve, half_ready, at(g, 2, hb + 1))
                nc.vector.tensor_copy(hl[:, b, :, 0, :], xn[:, b, :, 0, :]).then_inc(half_ready, 1)
                wait(dve, half_ready, at(g, 2, hb + 2))
                nc.vector.tensor_tensor(hl[:, b, :, 1, :], xn[:, b, :, 0, :], hl[:, b, :, 0, :],
                                        ALU.subtract).then_inc(norm_ready, 1)

            def gate(t, residual_high=None):
                b = t[1] % 2
                done = [0]

                def step(ins):
                    done[0] += 1
                    ins.then_inc(gate_step, 1)

                def after():
                    wait(dve, gate_step, at(t, GATE, done[0]))
                gl = ring[1][:, 0:TG * 2 * E].rearrange("p (t k e) -> p t k e", t=TG, k=2)
                wait(dve, gate_done, at(t, 1, 1))
                step(nc.vector.scalar_tensor_tensor(lg[:, b], gl[:, :, 0], 1.0 / (XS * WS),
                                                    bg_sb[:].unsqueeze(1).broadcast_to([P, TG, E]), ALU.mult, ALU.add))
                after()
                step(nc.vector.scalar_tensor_tensor(lg[:, b], gl[:, :, 1], 1.0 / (XS * WS), lg[:, b], ALU.mult, ALU.add))
                after()
                if residual_high:
                    residual_high()
                for v in range(TG):
                    step(nc.vector.max(top[:, b, v], lg[:, b, v]))
                after()
                step(nc.vector.tensor_tensor(gap[:, b], top[:, b, :, 1], top[:, b, :, 0], ALU.subtract))
                for v in range(TG):
                    step(nc.vector.max_index(topi[:, b, v], top[:, b, v], lg[:, b, v]))
                after()
                step(nc.vector.tensor_copy(topf[:, b], topi[:, b, :, 0:2]))
                after()
                for k in range(2):
                    step(nc.vector.tensor_tensor(oh[:, b, k], iota8[:].unsqueeze(1).broadcast_to([P, TG, E]),
                                                 topf[:, b, :, k].unsqueeze(2).broadcast_to([P, TG, E]), ALU.is_equal))
                wait(dve, tanh_ready, at(t, 1, 1))
                for k in range(2):
                    step(nc.vector.tensor_scalar(w12[:, b, :, k], th[:, b], (-0.5, 0.5)[k], 0.5, ALU.mult, ALU.add))
                after()
                for k in range(2):
                    step(nc.vector.tensor_tensor(oh[:, b, k], oh[:, b, k],
                                                 w12[:, b, :, k].unsqueeze(2).broadcast_to([P, TG, E]), ALU.mult))
                after()
                step(nc.vector.tensor_tensor(wd[:, b], oh[:, b, 0], oh[:, b, 1], ALU.add))
                after()
                wait(dve, wt_done, at(t, 1, -1))
                step(nc.vector.tensor_copy(wdh[:, b, :, 0], wd[:, b]))
                after()
                step(nc.vector.tensor_tensor(wdh[:, b, :, 1], wd[:, b], wdh[:, b, :, 0], ALU.subtract))
                assert done[0] == GATE

            def second_xs(t):
                wait(dve, xt2_done, at(t, 1, 1))
                wait(dve, h_done, at(t, CH, -CH))
                nc.vector.tensor_copy(xs2[:, t[1] % 2], half(ring[0])).then_inc(xs2_ready, 1)

            first, second = (None, 0), (None, 1)

            def body(g):
                nxt, prv2, nn = sh(g, 1), sh(g, -2), sh(g, 2)
                if is_step(g, -1):
                    dve.wait_ge(wvo_done, 1)
                    nc.vector.tensor_scalar(wvo[:], banks[0][:, 0:PAIRS * C].rearrange("p (a c) -> p a c", a=PAIRS),
                                            WS, None, ALU.mult).then_inc(wvo_ready, 1)
                if is_step(g, 0):
                    dve.wait_ge(cols_done, 1)
                    nc.vector.tensor_copy(cols[:], banks[1][:, 0:23]).then_inc(cols_ready, 1)
                    link(nc.vector.memset(ybias[:], 0.0))
                    dve.wait_ge(cw_done, 2)
                    dve.wait_ge(cols_ready, 1)
                    nc.vector.tensor_tensor(ybias[0:C, :], banks[1][0:C, 256:257], cols[0:C, 22:23], ALU.add).then_inc(ybias_ready, 1)
                    dve.wait_ge(cw_ready, 2)
                    cvt = cv32[:].rearrange("p (t c) -> p t c", t=TAPS)
                    nc.vector.tensor_copy(cv[0:C, :, 0, :], cvt).then_inc(cv_ready, 1)
                    dve.wait_ge(cv_ready, 1)
                    nc.vector.tensor_tensor(cv[0:C, :, 1, :], cvt, cv[0:C, :, 0, :], ALU.subtract).then_inc(cv_ready, 1)
                if is_step(g, 2):
                    dve.wait_ge(half_ready, NT + 2 * 4)
                    rsqrt(EPS_C, 2, QT, NT)
                if is_step(g, 3):
                    dve.wait_ge(ffnw, 16 * 6)
                    link(nc.vector.tensor_scalar(wg_sb[:], wg_sb[:], WS, None, ALU.mult))
                    link(nc.vector.tensor_copy(wg_hl[:, 0], wg_sb[:]))
                    nc.vector.tensor_tensor(wg_hl[:, 1], wg_sb[:], wg_hl[:, 0], ALU.subtract).then_inc(gatew_ready, 1)
                    dve.wait_ge(idn, 3)
                    nc.vector.tensor_tensor(
                        sel[:].rearrange("k p (e c) -> k (p e) c", e=2),
                        ident[0:2 * E, 0:E].unsqueeze(2).broadcast_to([2 * E, E, C]),
                        ident[0:2 * E, E:2 * E].unsqueeze(2).broadcast_to([2 * E, E, C]), ALU.add).then_inc(gatew_ready, 1)
                if is_step(g, NG - 1):
                    dve.wait_ge(st_ready, N2 // TG)
                    rsqrt(EPS_T, 3, 0, N2)
                for u in range(TG):
                    t, v = tile(g, u)
                    if real(t):
                        src = dots[v % 2][:].rearrange("p (h j) -> p h j", h=HEADS)
                        wait(dve, dots_done, at(t, TG, v + 1))
                        nc.vector.tensor_reduce(mx[:, v % 2], src, axis=AX.X, op=ALU.max).then_inc(mx_ready, 1)
                        wait(dve, mx_ready, at(t, TG, v + 1))
                        wait(dve, exp_ready, at(t, TG, v - 1))
                        nc.vector.tensor_tensor(sc[:, v % 2], src, mx[:, v % 2].unsqueeze(2).broadcast_to([P, HEADS, WT]),
                                                ALU.subtract).then_inc(sub_ready, 1)
                    t, v = tile(g, u - 1)
                    if real(t):
                        wait(dve, exp_ready, at(t, TG, v + 1))
                        nc.vector.reduce_sum(sm[:, v % 2], pe_[:, v % 2], axis=AX.X).then_inc(sum_ready, 1)
                        wait(dve, sum_ready, at(t, TG, v + 1))
                        wait(dve, pn_ready, at(t, TG, v - 1))
                        nc.vector.reciprocal(rs[:, v % 2], sm[:, v % 2]).then_inc(rs_ready, 1)
                    if u == 1 and real(nxt):
                        b = nxt[1] % 2
                        src = turn[XT32][:].rearrange("p (t y n c) -> p t y n c", t=TG, y=WSZ, n=2)
                        dst = bd[:, b].rearrange("p (t n) k (y c) -> p t y n k c", n=2, y=WSZ)
                        wait(dve, xt32_done, at(nxt, 1, 1))
                        wait(dve, dots_done, at(nxt, TG, -TG))
                        if is_step(nxt, 0):
                            dve.wait_ge(zeroed, 2)
                        for k in range(2):
                            nc.vector.tensor_copy(dst[k * C:(k + 1) * C, :, :, :, k, :], src[k * C:(k + 1) * C]).then_inc(bd_ready, 1)
                    if u == 2 and real(prv2):
                        src = turn[YT][:].rearrange("p (t k c) -> p t k c", t=TG, k=2)
                        b = prv2[1] % 2
                        wait(dve, yt_done, at(prv2, 1, 1))
                        xs = x_sb[:, bass.ds(idx(prv2, TG), TG), :]
                        xd = x1[:, bass.ds(idx(prv2, TG), TG), :]
                        nc.vector.tensor_tensor(tmp[:, b], src[:, :, 0], xs, ALU.add).then_inc(x1_ready, 1)
                        wait(dve, x1_ready, at(prv2, 2, 1))
                        nc.vector.tensor_tensor(xd, src[:, :, 1], tmp[:, b], ALU.add).then_inc(x1_ready, 1)
                        wait(dve, x1_ready, at(prv2, 2, 2))
                        for v in range(TG):
                            ins = nc.vector.bn_stats(st[:, idx(prv2, TG, v), :], x1[:, idx(prv2, TG, v), :])
                        ins.then_inc(st_ready, 1)
                    if u == 0 and real(g):
                        for k in range(2):
                            wait(dve, bt_done, at(g, 2, k + 1))
                            wait(dve, z_done, at(g, TG, -TG))
                            nc.vector.tensor_copy(bt[:, g[1] % 2, k * TG:(k + 1) * TG],
                                                  turn[BTA + k][:].rearrange("p (a b) -> p a b", a=TG)).then_inc(bt_ready, 1)
                    if is_step(g, 1) and u < 3:
                        statistics(u + 1)
                    if is_step(g, NG - 1) and u == 3:
                        normalise(first, x1, False, NT + 2 * NG)
                    if is_step(g, NG):
                        if u == 0:
                            second_xs(first)
                        if u == 1:
                            gate(first)
                        if u == 3:
                            normalise(second, x1, False, NT + 2 * NG)
                    if u == 3:
                        if real(nn):
                            wait(dve, xt32_done, at(nn, 1, -1))
                            normalise(nn, x_sb, True, QT if g[0] is None and g[1] < 1 else NT)
            steps(dve, body, -2, NG + 1)

            def experts(g):
                nxt, nn, prv = sh(g, 1), sh(g, 2), sh(g, -1)
                if is_step(g, 1):
                    dve.wait_ge(st_ready, NG)
                    rsqrt(EPS_T, 4, N2, NT)

                def pair_out(t, p):
                    wait(dve, ffn2_done, at(t, CH // 2, 2 * p + 2))
                    wait(dve, wb_ready, at(t, EP, p + 1))
                    wait(dve, acc_ready, at(t, 3, (-2, -2, -1, 0)[p]))
                    nc.vector.scalar_tensor_tensor(yw[:, p], outb[p % 2][:], cols[:, 16 + p:17 + p], wb[:, t[1] % 2, p],
                                                   ALU.add, ALU.mult).then_inc(yw_ready, 1)

                halves = ring[0][:].rearrange("p (t k c) -> p t k c", t=TG, k=2)

                def residual_high():
                    wait(dve, f_done, at(prv, 1, 1))
                    nc.vector.tensor_tensor(tmp[:, prv[1] % 2], halves[:, :, 0], x1[:, bass.ds(idx(prv, TG), TG), :],
                                            ALU.add).then_inc(o_step, 1)

                for j in range(CH // 2):
                    if j == 0:
                        if real(prv):
                            pair_out(prv, 3)
                        if real(nxt):
                            second_xs(nxt)
                    if j in (2, 4, 6) and real(g):
                        pair_out(g, j // 2 - 1)
                    if j == 3:
                        if real(nxt):
                            gate(nxt, residual_high if real(prv) else None)
                        elif real(prv):
                            residual_high()
                        if real(prv):
                            b = prv[1] % 2
                            wait(dve, stored[b], at(sh(prv, -b), 8, 0))
                            wait(dve, o_step, at(prv, 1, 1))
                            nc.vector.tensor_tensor(ob[:, b], halves[:, :, 1], tmp[:, b], ALU.add).then_inc(out_ready, 1)
                    if j == 7 and real(nn):
                        wait(dve, xt2_done, at(nn, 1, -1))
                        normalise(nn, x1, False, NT + 2 * NG)
            steps(dve, experts, 0, NG)

        @block.tensor
        def _(pe):
            pe.wait_ge(wqkv_in, 48)
            pe.wait_ge(idn, 2)
            for bank, w in ((banks[0], wq_sb), (banks[1], wk_sb), (banks[2], wv_sb)):
                for h in range(HEADS):
                    last = nc.tensor.transpose(bank[0:DK, h * C:(h + 1) * C], w[:, h * DK:(h + 1) * DK], ident[0:C, 0:C])
                if w is wk_sb:
                    last.then_inc(wT_done, 1)
            for k in range(2):
                last = nc.tensor.transpose(banks[3][:, k * C:(k + 1) * C], wv_sb[:, k * P:(k + 1) * P], ident[0:C, 0:C])
            last.then_inc(wT_done, 1)
            pe.wait_ge(qk_ready, 2)
            for h in range(HEADS):
                last = nc.tensor.matmul(banks[4][:, h * C:(h + 1) * C], wqT[:, h].rearrange("p a c -> p (a c)"), wkT[:, h],
                                        start=True, stop=True)
            last.then_inc(g_done, 1)
            pe.wait_ge(v_ready, 2)
            pe.wait_ge(idn, 3)
            pe.wait_ge(wout_in, 32)
            for h in range(HEADS):
                o = (h % 2) * C
                last = nc.tensor.matmul(banks[0][o:o + C, (h // 2) * C:(h // 2 + 1) * C], wvTh[:, h], wo_h[:, h],
                                        start=True, stop=True)
            last.then_inc(wvo_done, 1)

            def conv_weights():
                pe.wait_ge(wlocs, 32)
                for j in range(2):
                    for hf in range(2):
                        for ic in range(2):
                            last = nc.tensor.matmul(banks[2 + j][hf * C:(hf + 1) * C, :], wvT[:, ic],
                                                    wloc[:, ic, 4 * j + hf:4 * j + hf + 3:2, :], start=(ic == 0), stop=(ic == 1))
                    last.then_inc(vl_done, 1)
                pe.wait_ge(g_ready, 1)
                for ic in range(2):
                    last = nc.tensor.matmul(banks[4][0:C, 0:HC], wvT[:, ic], wloc[:, ic, TAPS - 1], start=(ic == 0), stop=(ic == 1))
                last.then_inc(vl_done, 1)
                pe.wait_ge(rows_in, 16 * 5)
                nc.tensor.transpose(banks[1][:, 0:23], rows[:], ident[0:23, 0:23]).then_inc(cols_done, 1)
                pe.wait_ge(wvo_ready, 1)
                for m in range(TP):
                    pe.wait_ge(vl_ready, m // 2 + 1)
                    if m == 2:
                        pe.wait_ge(vl_ready, 3)
                    n = P if m < TP - 1 else C
                    for k in range(2):
                        o = (m % 2) * 2 * P + k * n
                        last = nc.tensor.transpose(vltb[m // 2][:, o:o + n], vl[0:n, m, k * P:(k + 1) * P], ident[0:n, 0:n])
                    if m % 2 == 1 or m == TP - 1:
                        last.then_inc(vlT_done, 1)
                pe.wait_ge(cols_ready, 1)
                for k in range(2):
                    nc.tensor.matmul(banks[1][0:C, 256:257], wo_sb[:, k], cols[:, 20 + k:21 + k], start=(k == 0), stop=(k == 1))
                for k in range(TAPS):
                    pe.wait_ge(vlT_ready, k // 4 + 1)
                    for oc in range(2):
                        last = nc.tensor.matmul(banks[4 if k < 8 else 3][0:C, (k % 8) * C:(k % 8 + 1) * C],
                                                vlT[:, k // 2, oc, (k % 2) * C:(k % 2 + 1) * C], wo_sb[:, oc],
                                                start=(oc == 0), stop=(oc == 1))
                    if k >= 7:
                        last.then_inc(cw_done, 1)
                pe.wait_ge(cw_ready, 2)
                pe.wait_ge(ybias_ready, 1)

            def do_a(nxt, pr):
                b = nxt[1] % 2
                bank = turn[a_turn[pr]]
                rhs = xsp[:, b, :, 1:1 + HI, 1:1 + WI]
                for hv, wsp in enumerate((g_hi, g_lo)):
                    last = nc.tensor.matmul(bank[:], wsp[:, pr * P:(pr + 1) * P], rhs, start=(hv == 0), stop=(hv == 1))
                last.then_inc(a_done, 1)

            def second_xt(t):
                wait(pe, norm_ready, at(t, 1, NG + 1))
                wait(pe, wb_ready, at(t, EP, -1))
                for k in range(TG):
                    last = nc.tensor.transpose(half(ring[0])[:, k * P:(k + 1) * P],
                                               hl[:, t[1] % 2, k].rearrange("p a c -> p (a c)"), ident16[:])
                last.then_inc(xt2_done, 1)

            def gate_logits(t):
                wait(pe, xs2_ready, at(t, 1, 1))
                wait(pe, wb_ready, at(t, EP, 0))
                for v in range(TG):
                    last = nc.tensor.matmul(ring[1][:, v * 2 * E:(v + 1) * 2 * E], xs2[:, t[1] % 2, v * P:(v + 1) * P],
                                            wg_hl[:].rearrange("p k e -> p (k e)"), start=True, stop=True)
                last.then_inc(gate_done, 1)

            def weights_t(t):
                wait(pe, gate_step, at(t, GATE, GATE))
                for k in range(TG):
                    last = nc.tensor.transpose(half(ring[1])[0:2 * E, k * P:(k + 1) * P],
                                               wdh[:, t[1] % 2, k].rearrange("p a e -> p (a e)"), ident16[:])
                last.then_inc(wt_done, 1)

            def spread(t, p):
                wait(pe, wt_ready, at(t, 1, 1))
                if p == 0:
                    wait(pe, out_ready, at(sh(t, -2), 1, 1))
                wait(pe, wb_ready, at(t, EP, p - 1))
                nc.tensor.matmul(ring[p % 2][:], sel[:, p], wdT[:, t[1] % 2], start=True, stop=True).then_inc(wb_done, 1)

            first = (None, 0)

            def body(g):
                nxt, prv, prv2 = sh(g, 1), sh(g, -1), sh(g, -2)
                if is_step(g, 0):
                    conv_weights()
                if is_step(g, NG):
                    pe.wait_ge(gatew_ready, 2)
                    pe.wait_ge(bt_ready, 2 * NG)
                for u in range(TG):
                    t, v = tile(g, u)
                    if real(t):
                        b = t[1] % 2
                        if v == 0:
                            wait(pe, a_ready, at(t, PAIRS, PAIRS))
                            wait(pe, bd_ready, at(t, 2, 2))
                        wait(pe, sub_ready, at(t, TG, v - 1))
                        for pr in range(PAIRS):
                            for w in range(2):
                                last = nc.tensor.matmul(
                                    dots[v % 2][w * WT:(w + 1) * WT, pr * P:(pr + 1) * P],
                                    aa[:, b, pr, w * TG * WT + v * WT:w * TG * WT + (v + 1) * WT],
                                    bd[:, b, 2 * v + w].rearrange("p a j -> p (a j)"), start=True, stop=True)
                        last.then_inc(dots_done, 1)
                    nb = nxt[1] % 2
                    if u == 0 and real(g):
                        for k in range(2):
                            if k == 0 and real(sh(g, -3)):
                                wait(pe, x1_ready, at(sh(g, -3), 2, 2))
                            if k == 1:
                                wait(pe, a_ready, at(g, PAIRS, 3))
                            for a in range(TG):
                                last = nc.tensor.transpose(turn[BTA + k][:, a * P:(a + 1) * P],
                                                           bd[:, g[1] % 2, k * TG + a].rearrange("p a j -> p (a j)"), ident[:])
                            last.then_inc(bt_done, 1)
                    if u == 1:
                        if real(prv):
                            wait(pe, y_ready, at(prv, 1, 0))
                            if is_step(prv, 0):
                                pe.wait_ge(cv_in, 16)
                            for k in range(TAPS):
                                rhs = xsp[:, prv[1] % 2, :, k // 3:k // 3 + HI, k % 3:k % 3 + WI]
                                last = nc.tensor.matmul(attb[:], cv[:, k].rearrange("p a c -> p (a c)"), rhs,
                                                        start=(k == 0), stop=False, skip_group_check=True)
                            last.then_inc(conv_done, 1)
                        if is_step(g, NG):
                            gate_logits(first)
                        if real(nxt):
                            wait(pe, norm_ready, at(nxt, 1, 1))
                            wait(pe, a_ready, at(nxt, PAIRS, 0))
                            for k in range(TG):
                                last = nc.tensor.transpose(half(turn[X16])[:, k * P:(k + 1) * P],
                                                           hl[:, nb, k].rearrange("p a c -> p (a c)"), ident16[:])
                            last.then_inc(x16_done, 1)
                            wait(pe, bt_ready, at(nxt, 2, -1))
                            for k in range(TG):
                                last = nc.tensor.transpose(turn[XT32][:, k * P:(k + 1) * P],
                                                           xn[:, nb, k].rearrange("p a c -> p (a c)"), ident[:])
                            last.then_inc(xt32_done, 1)
                    if u == 2:
                        if real(nxt):
                            if is_step(nxt, 0):
                                pe.wait_ge(g_ready, 1)
                            wait(pe, xsp_ready, at(nxt, 1, 1))
                            wait(pe, bt_ready, at(nxt, 2, 0))
                            do_a(nxt, 0)
                            do_a(nxt, 1)
                        if real(prv2):
                            if real(nxt):
                                wait(pe, bd_ready, at(nxt, 2, 2))
                            else:
                                wait(pe, bt_ready, 2 * NG)
                                wait(pe, x1_ready, at(prv2, 2, 0))
                            wait(pe, y_ready, at(prv2, 1, 1))
                            for k in range(TG):
                                last = nc.tensor.transpose(turn[YT][:, k * P:(k + 1) * P], ys[:, prv2[1] % 2, k * P:(k + 1) * P], ident[:])
                            last.then_inc(yt_done, 1)
                    if u == 0 and is_step(g, NG):
                        second_xt(first)
                    if u == 3:
                        if is_step(g, NG):
                            weights_t(first)
                        if real(nxt):
                            wait(pe, a_ready, at(nxt, PAIRS, 1))
                            do_a(nxt, 2)
                            wait(pe, a_ready, at(nxt, PAIRS, 2))
                            do_a(nxt, 3)
                        if real(prv):
                            wait(pe, z_ready, at(prv, TG, TG))
                            for k in range(2):
                                for hf in range(2):
                                    pr = 2 * hf + k
                                    last = nc.tensor.matmul(attb[hf * C:(hf + 1) * C, :], wvo[:, pr], zs[:, prv[1] % 2, :, pr, :],
                                                            start=False, stop=(k == 1), skip_group_check=True)
                            last.then_inc(att_done, 1)
                        if is_step(g, NG):
                            for p in range(EP):
                                spread(first, p)
                    t, v = tile(g, u - 2)
                    if real(t):
                        wait(pe, pn_ready, at(t, TG, v + 1))
                        wait(pe, pt_ready, at(t, TG, v))
                        for pr in range(PAIRS):
                            last = nc.tensor.transpose(ptb[:, pr * P:(pr + 1) * P], pn[:, v % 2, pr * P:(pr + 1) * P], ident[:])
                        last.then_inc(pt_done, 1)
                    t, v = tile(g, u - 3)
                    if real(t):
                        wait(pe, pt_ready, at(t, TG, v + 1))
                        wait(pe, bt_ready, at(t, 2, 2))
                        wait(pe, z_ready, at(t, TG, v))
                        zo = zb[:].rearrange("p (a y n c) -> p a y n c", a=PAIRS, y=WSZ, n=2)
                        for w in range(2):
                            last = nc.tensor.matmul(zo[:, :, :, w, :], bt[:, t[1] % 2, 2 * v + w],
                                                    pt[:, v % 2, :, w * WT:(w + 1) * WT], start=True, stop=True)
                        last.then_inc(z_done, 1)
            steps(pe, body, -1, NG + 1)

            pe.wait_ge(w1_ready, 3)

            def experts(g):
                nxt, prv = sh(g, 1), sh(g, -1)

                def ffn2(t, j):
                    for c in (2 * j, 2 * j + 1):
                        e, k = expert(c)
                        hf = (e % 2) * C
                        wait(pe, gelu_ready, at(t, CH, c + 1))
                        if k == 0 and c % 2 == 0:
                            wait(pe, yw_ready, at(t, EP, c // 4 - 1))
                        last = nc.tensor.matmul(outb[(c // 4) % 2][hf:hf + C, :], w2_sb[:, e, k], hh[:, c % 4],
                                                start=(k == 0), stop=(k == 1))
                    last.then_inc(ffn2_done, 1)

                for j in range(CH // 2):
                    if real(g):
                        for c in (2 * j, 2 * j + 1):
                            e, k = expert(c)
                            if c == 0:
                                wait(pe, xs2_ready, at(g, 1, 1))
                            wait(pe, gelu_ready, at(g, CH, c - 3))
                            o = (2 * e + k) * P
                            nc.tensor.matmul(hidb[c % 4][:], w1_hi[:, o:o + P], xs2[:, g[1] % 2], start=True, stop=False)
                            nc.tensor.matmul(hidb[c % 4][:], w1_lo[:, o:o + P], xs2[:, g[1] % 2], start=False,
                                             stop=True).then_inc(h_done, 1)
                    if j == 0 and real(prv):
                        ffn2(prv, CH // 2 - 1)
                    if j > 0 and real(g):
                        ffn2(g, j - 1)
                    if j == 0 and real(nxt):
                        second_xt(nxt)
                    if j == 1 and real(nxt):
                        gate_logits(nxt)
                    if j == 3 and real(prv):
                        wait(pe, acc_ready, at(prv, 3, 3))
                        if not real(nxt):
                            wait(pe, out_ready, at(prv, 1, 0))
                            wait(pe, wb_ready, EP * NG)
                        for k in range(TG):
                            last = nc.tensor.transpose(ring[0][:, k * P:(k + 1) * P], acc[:, prv[1] % 2, k * P:(k + 1) * P], ident[:])
                        last.then_inc(f_done, 1)
                    if j == 5 and real(nxt):
                        weights_t(nxt)
                    if j in (6, 7) and real(nxt):
                        spread(nxt, 2 * (j - 6))
                        spread(nxt, 2 * (j - 6) + 1)
            steps(pe, experts, 0, NG)


_INS = ['x', 'L0_conv_w_q', 'L0_conv_w_k', 'L0_conv_w_v', 'L0_conv_w_local', 'L0_conv_b_local', 'L0_conv_w_out',
        'L0_conv_b_out', 'L0_ffn_Wg', 'L0_ffn_bg', 'L0_ffn_W1', 'L0_ffn_b1', 'L0_ffn_W2', 'L0_ffn_b2']


def kernel(**inputs):
    import concourse.bacc as bacc
    from concourse.bass_utils import run_bass_kernel_spmd

    nc = bacc.Bacc("TRN2", target_bir_lowering=False, num_devices=1)
    arrays, args = {}, []
    for name in _INS:
        a = np.ascontiguousarray(inputs[name])
        if name == 'x':
            a = a.reshape(B * HI * WI, C)
        arrays[f"in_{name}"] = a
        args.append(nc.dram_tensor(f"in_{name}", a.shape, mybir.dt.from_np(a.dtype), kind="ExternalInput").ap())
    args.append(nc.dram_tensor("out", (B * HI * WI, C), F32, kind="ExternalOutput").ap())
    program(nc, *args)
    r = run_bass_kernel_spmd(nc, [arrays], core_ids=[0])
    return r.results[0]["out"].reshape(B, HI, WI, C)
```

```python
import numpy as np

import concourse.bass as bass
from concourse import mybir
from contextlib import ExitStack

F32 = mybir.dt.float32
F16 = mybir.dt.float16
U32 = mybir.dt.uint32
ACT = mybir.ActivationFunctionType
ALU = mybir.AluOpType
AX = mybir.AxisListType

B, HI, WI, C = 32, 16, 16, 64
HEADS, DK, WSZ = 8, 32, 8
HC = HEADS * DK
E, HID = 8, 256
P = 128
WT = WSZ * WSZ
NT = B * HI * WI // P
TG = 4
NG = NT // TG
GT = TG * P
IG = GT // (HI * WI)
PAIRS = HEADS // 2
EP = E // 2
TAPS = 9
PADW = WI + 2
CH = E * HID // P
EPS_C, EPS_T = 1e-6, 1e-5
SCALE = DK ** -0.5
XS = 16.0
WS = 16.0


def at(g, per, extra):
    i, off = g
    static = off * per + extra
    return static if i is None else i * (2 * per) + static


def sh(g, d):
    return (g[0], g[1] + d)


def real(g):
    return g[0] is not None or 0 <= g[1] < NG


def is_step(g, s):
    return g[0] is None and g[1] == s


def tile(g, u):
    return sh(g, u // TG), u % TG


def idx(g, per, extra=0):
    return at(g, per, extra)


def wait(eng, sem, value):
    if isinstance(value, int) and value <= 0:
        return
    eng.wait_ge(sem, value)


def steps(eng, body, first, last):
    for s in range(first, 4):
        body((None, s))
    with eng.Fori(2, NG // 2 - 1) as i:
        body((i, 0))
        body((i, 1))
    for s in range(NG - 2, last + 1):
        body((None, s))


def expert(c):
    return 2 * (c // 4) + c % 2, (c % 4) // 2


N2 = NT - 4 * TG
TP = (TAPS + 1) // 2
QT = NT // 4
LOADS = (0, QT // 2, QT, 2 * QT, 3 * QT, NT)
GATE = 21


def program(nc, x, w_q, w_k, w_v, w_local, b_local, w_out, b_out, wg, bg, w1, b1, w2, b2, out):
    ctx = ExitStack()
    with ctx:
        def sb(name, shape, dt=F32):
            return ctx.enter_context(nc.sbuf_tensor(name, shape, dt))

        def sem(name):
            return ctx.enter_context(nc.semaphore(name))

        ident = sb("ident", [P, P])
        ident16 = sb("ident16", [P, P], F16)
        swap16 = sb("swap16", [P, P], F16)
        both16 = sb("both16", [P, 2, C], F16)
        par = sb("par", [P, 2])
        iota8 = sb("iota8", [P, E])
        sel = sb("sel", [2 * E, EP, P], F16)
        wq_sb = sb("wq_sb", [C, HC])
        wk_sb = sb("wk_sb", [C, HC])
        wv_sb = sb("wv_sb", [C, HC])
        wqT = sb("wqT", [DK, HEADS, 2, C])
        wkT = sb("wkT", [DK, HEADS, C])
        wvTh = sb("wvTh", [DK, HEADS, C])
        wvT = sb("wvT", [P, 2, C])
        wloc = sb("wloc", [P, 2, TAPS, HC])
        wo_sb = sb("wo_sb", [P, 2, C])
        wo_h = sb("wo_h", [DK, HEADS, C])
        vl = sb("vl", [P, TP, HC])
        vlT = sb("vlT", [P, TP, 2, P])
        rows = sb("rows", [23, P])
        cols = sb("cols", [P, 23])
        ybias = sb("ybias", [P, 1])
        bg_sb = sb("bg_sb", [P, E])
        g32 = sb("g32", [P, HEADS * C])
        g_hi = sb("g_hi", [P, HEADS * C], F16)
        g_lo = sb("g_lo", [P, HEADS * C], F16)
        cv32 = sb("cv32", [C, TAPS * C])
        cv = sb("cv", [P, TAPS, 2, C], F16)
        wvo = sb("wvo", [P, PAIRS, C])
        w1_sb = sb("w1_sb", [P, E * HID])
        w1_hi = sb("w1_hi", [P, E * HID], F16)
        w1_lo = sb("w1_lo", [P, E * HID], F16)
        wg_sb = sb("wg_sb", [P, E])
        wg_hl = sb("wg_hl", [P, 2, E], F16)
        w2_sb = sb("w2_sb", [P, E, 2, C])
        x_sb = sb("x_sb", [P, NT, C])
        x1 = sb("x1", [P, NT, C])
        st = sb("st", [P, NT, 6])
        mean = sb("mean", [P, NT])
        rstd = sb("rstd", [P, NT])
        va = sb("va", [P, NT])
        vb = sb("vb", [P, NT])
        vc = sb("vc", [P, NT])
        xn = sb("xn", [P, 2, TG, C])
        xc = sb("xc", [P, 2, TG, C])
        hl = sb("hl", [P, 2, TG, 2, C], F16)
        xsp = sb("xsp", [P, 2, IG, PADW, PADW], F16)
        bd = sb("bd", [P, 2, TG * 2, 2, WT])
        bt = sb("bt", [P, 2, TG * 2, P])
        aa = sb("aa", [P, 2, PAIRS, GT])
        sc = sb("sc", [P, 2, HEADS, WT])
        pe_ = sb("pe_", [P, 2, HEADS, WT])
        pn = sb("pn", [P, 2, HEADS * WT])
        pt = sb("pt", [P, 2, PAIRS, P])
        mx = sb("mx", [P, 2, HEADS])
        sm = sb("sm", [P, 2, HEADS])
        rs = sb("rs", [P, 2, HEADS])
        zs = sb("zs", [P, 2, TG, PAIRS, P])
        ys = sb("ys", [P, 2, GT])
        tmp = sb("tmp", [P, 2, TG, C])
        xs2 = sb("xs2", [P, 2, GT], F16)
        lg = sb("lg", [P, 2, TG, E])
        top = sb("top", [P, 2, TG, 8])
        topi = sb("topi", [P, 2, TG, 8], U32)
        topf = sb("topf", [P, 2, TG, 2])
        gap = sb("gap", [P, 2, TG])
        th = sb("th", [P, 2, TG])
        w12 = sb("w12", [P, 2, TG, 2])
        oh = sb("oh", [P, 2, 2, TG, E])
        wd = sb("wd", [P, 2, TG, E])
        wdh = sb("wdh", [P, 2, TG, 2, E], F16)
        wdT = sb("wdT", [2 * E, 2, GT], F16)
        wb = zs[:].rearrange("p b t a c -> p b t (a c)")
        wl = wloc[:].rearrange("p k t o -> p k (t o)")
        hh = wl[:, 0, 0:4 * GT].rearrange("p (a b) -> p a b", a=4)
        yw = wl[:, 1, 0:EP * GT].rearrange("p (a b) -> p a b", a=EP)
        acc = sb("acc", [P, 2, GT])
        ob = sb("ob", [P, 2, TG, C])

        banks = [ctx.enter_context(nc.psum_tensor(f"bank{i}", [P, 512], F32)) for i in range(8)]

        wqk_in = sem("wqk_in")
        wv_in = sem("wv_in")
        wout_in = sem("wout_in")
        wloc_in = sem("wloc_in")
        rows_in = sem("rows_in")
        ffn_in = sem("ffn_in")
        x_in = [sem(f"x_in{i}") for i in range(len(LOADS) - 1)]
        ident_ready = sem("ident_ready")
        wT_done = sem("wT_done")
        qk_ready = sem("qk_ready")
        v_ready = sem("v_ready")
        g_done = sem("g_done")
        g_ready = sem("g_ready")
        wvo_done = sem("wvo_done")
        wvo_ready = sem("wvo_ready")
        vl_done = sem("vl_done")
        vl_ready = sem("vl_ready")
        cols_done = sem("cols_done")
        cols_ready = sem("cols_ready")
        vlT_done = sem("vlT_done")
        vlT_ready = sem("vlT_ready")
        ybias_done = sem("ybias_done")
        cw_done = sem("cw_done")
        cw_ready = sem("cw_ready")
        ybias_ready = sem("ybias_ready")
        cv_ready = sem("cv_ready")
        cv_in = sem("cv_in")
        gatew_ready = sem("gatew_ready")
        dve_step = sem("dve_step")
        pool_step = sem("pool_step")
        w1_high = sem("w1_high")
        w1_ready = sem("w1_ready")
        sq_in = sem("sq_in")
        sq_done = sem("sq_done")
        zeroed = sem("zeroed")
        norm_ready = sem("norm_ready")
        x16_done = sem("x16_done")
        xt_done = sem("xt_done")
        xsp_ready = sem("xsp_ready")
        bd_ready = sem("bd_ready")
        a_done = sem("a_done")
        a_ready = sem("a_ready")
        xswap_done = sem("xswap_done")
        bt_ready = sem("bt_ready")
        dots_done = sem("dots_done")
        mx_ready = sem("mx_ready")
        sub_ready = sem("sub_ready")
        exp_ready = sem("exp_ready")
        sum_ready = sem("sum_ready")
        rs_ready = sem("rs_ready")
        pn_ready = sem("pn_ready")
        pt_done = sem("pt_done")
        pt_ready = sem("pt_ready")
        z_done = sem("z_done")
        z_ready = sem("z_ready")
        conv_done = sem("conv_done")
        att_done = sem("att_done")
        y_ready = sem("y_ready")
        yt_done = sem("yt_done")
        x1_ready = sem("x1_ready")
        half_ready = sem("half_ready")
        xn_ready = sem("xn_ready")
        stats1_ready = sem("stats1_ready")
        par_ready = sem("par_ready")
        rstd_ready = sem("rstd_ready")
        stats2_ready = sem("stats2_ready")
        xt2_done = sem("xt2_done")
        xs2_ready = sem("xs2_ready")
        gate_done = sem("gate_done")
        gate_step = sem("gate_step")
        tanh_ready = sem("tanh_ready")
        wt_done = sem("wt_done")
        wt_ready = sem("wt_ready")
        wb_done = sem("wb_done")
        wb_ready = sem("wb_ready")
        h_done = sem("h_done")
        gelu_ready = sem("gelu_ready")
        ffn2_done = sem("ffn2_done")
        yw_ready = sem("yw_ready")
        acc_ready = sem("acc_ready")
        f_done = sem("f_done")
        o_step = sem("o_step")
        out_ready = sem("out_ready")
        stored = [sem(f"stored{i}") for i in range(2)]

        block = ctx.enter_context(nc.Block())

        x_tiles = x.rearrange("(t p) d -> p t d", p=P)
        out_tiles = out.rearrange("(t p) d -> p t d", p=P)

        dots = [banks[0], banks[1]]
        ptb, zb = banks[2], banks[3]
        attb = banks[4]
        XSWAP, X16, XT, A0, A1, YT, A2, A3 = range(8)
        turn = [banks[5 + (k + 1) % 3] for k in range(8)]
        a_turn = (A0, A1, A2, A3)
        hidb = [banks[i] for i in range(4)]
        outb = [banks[4], banks[5]]
        ring = [banks[6], banks[7]]

        vlb = [banks[4], banks[3], banks[4]]
        vltb = [banks[3], banks[4], banks[3]]

        def w1_part(u):
            return slice(u * E * HID // 4, (u + 1) * E * HID // 4)

        def half(bank):
            return bank[:, 0:256].bitcast(F16)

        @block.sync
        def _(sp):
            def load_x(k):
                tiles = slice(LOADS[k], LOADS[k + 1])
                sp.dma_start(x_sb[:, tiles, :], x_tiles[:, tiles, :]).then_inc(x_in[k], 16)

            sp.dma_start(wq_sb[:], w_q[0, 0]).then_inc(wqk_in, 16)
            sp.dma_start(wk_sb[:], w_k[0, 0]).then_inc(wqk_in, 16)
            load_x(0)
            sp.dma_start(wv_sb[:], w_v[0, 0]).then_inc(wv_in, 16)
            load_x(1)
            sp.dma_start(rows[0:16, :], b1.rearrange("e (k n) -> (e k) n", n=P)).then_inc(rows_in, 16)
            sp.dma_start(rows[16:20, :], b2.rearrange("(p e) n -> p (e n)", e=2)).then_inc(rows_in, 16)
            sp.dma_start(rows[20:22, :], b_local.rearrange("(k n) -> k n", n=P)).then_inc(rows_in, 16)
            for k in range(2):
                sp.dma_start(rows[22:23, k * C:(k + 1) * C], b_out.unsqueeze(0)).then_inc(rows_in, 16)
            for k in range(2):
                sp.dma_start(wloc[:, k], w_local.rearrange("a b i o -> i (a b) o")[k * P:(k + 1) * P]).then_inc(wloc_in, 16)
            for k in range(2, len(LOADS) - 1):
                load_x(k)
            sp.dma_start(bg_sb[:], bg.unsqueeze(0).broadcast_to([P, E])).then_inc(ffn_in, 16)
            for h in range(2):
                sp.dma_start(wg_sb[h * C:(h + 1) * C, :], wg).then_inc(ffn_in, 16)
            for h in range(2):
                sp.dma_start(w1_sb[h * C:(h + 1) * C, :].rearrange("c (e n) -> c e n", e=E),
                             w1.rearrange("e c n -> c e n")).then_inc(ffn_in, 16)
            sp.dma_start(w2_sb[:], w2.rearrange("e (k n) c -> n e k c", n=P)).then_inc(ffn_in, 16)

            sp.wait_ge(cv_ready, 2)
            sp.dma_start(cv[C:P], cv[0:C]).then_inc(cv_in, 16)

            def body(g):
                prv = sh(g, -1)
                if real(prv):
                    b = prv[1] % 2
                    wait(sp, out_ready, at(prv, 1, 1))
                    sp.dma_start(out_tiles[:, bass.ds(idx(prv, TG), TG), :], ob[:, b]).then_inc(stored[b], 16)
            steps(sp, body, 0, NG)
            for b in range(2):
                sp.wait_ge(stored[b], 16 * (NG // 2))

        @block.gpsimd
        def _(pool):
            nc.gpsimd.memset(ident[:], 0.0).then_inc(pool_step, 1)
            nc.gpsimd.iota(iota8[:], [[1, E]], base=0, channel_multiplier=0,
                           allow_small_or_imprecise_dtypes=True).then_inc(ident_ready, 1)
            pool.wait_ge(pool_step, 1)
            nc.gpsimd.affine_select(out=ident[:], in_=ident[:], compare_op=ALU.not_equal, fill=1.0, base=0,
                                    pattern=[[-1, P]], channel_multiplier=1).then_inc(ident_ready, 1)
            pool.wait_ge(ident_ready, 2)
            nc.gpsimd.tensor_copy(ident16[:], ident[:]).then_inc(ident_ready, 1)
            for w in range(2):
                pool.wait_ge(ident_ready, 3 + w)
                nc.gpsimd.tensor_copy(swap16[:].rearrange("p (a n c) -> p a n c", n=2, c=WSZ)[:, :, w],
                                      ident16[:].rearrange("p (a n c) -> p a n c", n=2, c=WSZ)[:, :, 1 - w]).then_inc(ident_ready, 1)
            for k in range(2):
                rows_k = slice(k * C, (k + 1) * C)
                pool.wait_ge(ident_ready, 5 + k)
                nc.gpsimd.tensor_copy(both16[rows_k], ident16[rows_k, rows_k].unsqueeze(1).broadcast_to([C, 2, C])).then_inc(ident_ready, 1)
            pool.wait_ge(ident_ready, 7)
            nc.gpsimd.memset(xsp[:], 0.0).then_inc(zeroed, 1)
            nc.gpsimd.memset(bd[:], 0.0).then_inc(zeroed, 1)

            def before_normalise(g, u):
                if u == 1:
                    wait(pool, norm_ready, at(g, 1, 0))
                    wait(pool, bt_ready, at(g, 4, -4))
                    if is_step(g, 2):
                        pool.wait_ge(rstd_ready, 2)
                    if is_step(g, 4):
                        pool.wait_ge(rstd_ready, 3)
                if u == 2:
                    wait(pool, half_ready, at(g, 2, 1))
                    wait(pool, x16_done, at(g, 1, -1))
                    wait(pool, xswap_done, at(g, 1, -1))

            def normalise(g, u):
                b = g[1] % 2

                def of_tile(a):
                    return a[:, bass.ds(idx(g, TG), TG)].unsqueeze(2).broadcast_to([P, TG, C])
                if u == 1:
                    nc.gpsimd.tensor_tensor(xc[:, b], x_sb[:, bass.ds(idx(g, TG), TG), :], of_tile(mean), ALU.subtract).then_inc(half_ready, 1)
                if u == 2:
                    nc.gpsimd.tensor_tensor(xn[:, b], xc[:, b], of_tile(rstd), ALU.mult).then_inc(xn_ready, 1)
                    nc.gpsimd.tensor_tensor(hl[:, b, :, 0, :], xc[:, b], of_tile(rstd), ALU.mult).then_inc(half_ready, 1)
                if u == 3:
                    wait(pool, xn_ready, at(g, 1, -1))
                    wait(pool, half_ready, at(g, 2, 2))
                    nc.gpsimd.tensor_tensor(hl[:, b, :, 1, :], xn[:, b], hl[:, b, :, 0, :], ALU.subtract).then_inc(norm_ready, 1)

            def body(g):
                nn = sh(g, 2)
                for u in range(TG):
                    t, v = tile(g, u)
                    if not real(t):
                        continue
                    if real(nn):
                        before_normalise(nn, u)
                    wait(pool, rs_ready, at(t, TG, v + 1))
                    wait(pool, pt_done, at(t, TG, v - 1))
                    for k in range(2):
                        ins = nc.gpsimd.tensor_tensor(
                            pn[:, v % 2, :].rearrange("p (a y k c) -> p a k y c", a=PAIRS, k=2, c=WSZ)[:, :, k],
                            pe_[:, v % 2].rearrange("p (a k) (y c) -> p a k y c", k=2, c=WSZ)[:, :, k],
                            rs[:, v % 2, k::2].unsqueeze(2).unsqueeze(3).broadcast_to([P, PAIRS, WSZ, WSZ]), ALU.mult)
                    ins.then_inc(pn_ready, 1)
                    if real(nn):
                        normalise(nn, u)
            steps(pool, body, 0, NG - 1)

            def experts(g):
                if not real(g):
                    return
                b = g[1] % 2
                wait(pool, f_done, at(g, 1, -1))
                wait(pool, yw_ready, at(g, EP, 2))
                nc.gpsimd.tensor_tensor(acc[:, b], yw[:, 0], yw[:, 1], ALU.add).then_inc(acc_ready, 1)
                for p in (2, 3):
                    wait(pool, yw_ready, at(g, EP, p + 1))
                    wait(pool, acc_ready, at(g, 3, p - 1))
                    nc.gpsimd.tensor_tensor(acc[:, b], acc[:, b], yw[:, p], ALU.add).then_inc(acc_ready, 1)
            steps(pool, experts, 0, NG - 1)

        @block.scalar
        def _(act):
            act.dma_start(wo_h[:], w_out[0, 0].rearrange("(h d) o -> d h o", d=DK)).then_inc(wout_in, 16)
            act.dma_start(wo_sb[:], w_out[0, 0].rearrange("(k i) o -> i k o", i=P)).then_inc(wout_in, 16)

            act.wait_ge(wT_done, 1)
            nc.scalar.copy(wqT[:], banks[0][0:DK, :].rearrange("p (h c) -> p h c", h=HEADS)
                           .unsqueeze(2).broadcast_to([DK, HEADS, 2, C])).then_inc(qk_ready, 1)
            act.wait_ge(wT_done, 2)
            nc.scalar.copy(wvTh[:], banks[2][0:DK, :].rearrange("p (h c) -> p h c", h=HEADS)).then_inc(v_ready, 1)
            nc.scalar.copy(wvT[:], banks[3][:, 0:2 * C].rearrange("p (k c) -> p k c", k=2)).then_inc(v_ready, 1)
            act.wait_ge(sq_in, 1)
            nc.scalar.sqrt(vb[:, 0:QT // 2], va[:, 0:QT // 2]).then_inc(sq_done, 1)

            def gate_tanh(t):
                wait(act, gate_step, at(t, GATE, 7))
                nc.scalar.activation(th[:, t[1] % 2], gap[:, t[1] % 2], ACT.Tanh, scale=0.5).then_inc(tanh_ready, 1)

            def weights_out(t):
                wait(act, wt_done, at(t, 1, 1))
                wait(act, wb_done, at(t, EP, -EP))
                nc.scalar.copy(wdT[:, t[1] % 2], half(ring[1])[0:2 * E]).then_inc(wt_ready, 1)

            def spread_out(t, p):
                wait(act, wb_done, at(t, EP, p + 1))
                wait(act, yw_ready, at(t, EP, -EP))
                nc.scalar.copy(wb[:, t[1] % 2, p], ring[p % 2][:]).then_inc(wb_ready, 1)

            first = (None, 0)

            def conv_weights_out(u):
                if u == 0:
                    for j in range(2):
                        act.wait_ge(vl_done, j + 1)
                        nc.scalar.copy(vl[:, 2 * j:2 * j + 2], vlb[j][:].rearrange("p (m o) -> p m o", m=2)).then_inc(vl_ready, 1)
                if u == 1:
                    act.wait_ge(vl_done, 3)
                    nc.scalar.copy(vl[0:C, TP - 1], vlb[2][0:C, 0:HC]).then_inc(vl_ready, 1)
                for j in range(2):
                    if u == j + 1:
                        act.wait_ge(vlT_done, j + 1)
                        nc.scalar.copy(vlT[:, 2 * j:2 * j + 2], vltb[j][:].rearrange("p (m a c) -> p m a c", m=2, a=2)).then_inc(vlT_ready, 1)
                if u == 2:
                    act.wait_ge(vlT_done, 3)
                    nc.scalar.copy(vlT[:, TP - 1, :, 0:C], vltb[2][:, 0:2 * C].rearrange("p (a c) -> p a c", a=2)).then_inc(vlT_ready, 1)
                if u == 3:
                    act.wait_ge(cw_done, 1)
                    nc.scalar.mul(cv32[:, 8 * C:], banks[3][0:C, 0:C], WS).then_inc(cw_ready, 1)
                    act.wait_ge(cw_done, 2)
                    nc.scalar.mul(cv32[:, 0:8 * C], banks[4][0:C, :], WS).then_inc(cw_ready, 1)

            def body(g):
                nxt = sh(g, 1)
                for u in range(TG):
                    if real(nxt):
                        if u == 1:
                            wait(act, x16_done, at(nxt, 1, 1))
                            wait(act, conv_done, at(nxt, 1, -1))
                            if is_step(nxt, 0):
                                act.wait_ge(zeroed, 1)
                            b = nxt[1] % 2
                            src = half(turn[X16])
                            nc.scalar.copy(xsp[:, b, :, 1:1 + HI, 1:1 + WI],
                                           src.rearrange("p (m y c) -> p m y c", m=IG, y=HI)).then_inc(xsp_ready, 1)
                        if u in (2, 3):
                            for pr in (2 * (u - 2), 2 * (u - 2) + 1):
                                wait(act, a_done, at(nxt, PAIRS, pr + 1))
                                wait(act, dots_done, at(nxt, TG, -TG))
                                src = turn[a_turn[pr]]
                                dst = aa[:, nxt[1] % 2, pr, :].rearrange("p (n ty c) -> p ty n c", n=2, c=WSZ)
                                nc.scalar.mul(dst, src[:].rearrange("p (ty n c) -> p ty n c", n=2, c=WSZ),
                                              1.0 / WS).then_inc(a_ready, 1)
                    t, v = tile(g, u)
                    if real(t):
                        wait(act, sub_ready, at(t, TG, v + 1))
                        wait(act, pn_ready, at(t, TG, v - 1))
                        wait(act, sum_ready, at(t, TG, v - 1))
                        nc.scalar.activation(pe_[:, v % 2], sc[:, v % 2], ACT.Exp,
                                             scale=SCALE / XS / XS).then_inc(exp_ready, 1)
                    if is_step(g, 0):
                        conv_weights_out(u)
                    t, v = tile(g, u - 2)
                    if real(t):
                        wait(act, pt_done, at(t, TG, v + 1))
                        wait(act, z_done, at(t, TG, v - 1))
                        nc.scalar.copy(pt[:, v % 2], ptb[:].rearrange("p (a b) -> p a b", a=PAIRS)).then_inc(pt_ready, 1)
                    t, v = tile(g, u - 3)
                    if real(t):
                        wait(act, z_done, at(t, TG, v + 1))
                        wait(act, att_done, at(t, 1, -1))
                        nc.scalar.copy(zs[:, t[1] % 2, v], zb[:].rearrange("p (a b) -> p a b", a=PAIRS)).then_inc(z_ready, 1)
                    if is_step(g, NG) and u == 0:
                        gate_tanh(first)
                    if is_step(g, NG) and u == 2:
                        weights_out(first)
                    if is_step(g, -1) and u == 3:
                        act.wait_ge(sq_in, 2)
                        nc.scalar.sqrt(vb[:, QT // 2:QT], va[:, QT // 2:QT]).then_inc(sq_done, 1)
                    if is_step(g, 2) and u == 1:
                        act.wait_ge(sq_in, 3)
                        nc.scalar.sqrt(vb[:, QT:], va[:, QT:]).then_inc(sq_done, 1)
                    if is_step(g, NG - 2) and u == 1:
                        act.wait_ge(sq_in, 4)
                        nc.scalar.sqrt(vb[:, 0:N2], va[:, 0:N2]).then_inc(sq_done, 1)
                    if is_step(g, 3):
                        act.wait_ge(ffn_in, 16 * 6)
                        nc.scalar.mul(w1_hi[:, w1_part(u)], w1_sb[:, w1_part(u)], WS).then_inc(w1_high, 1)
                    prv = sh(g, -1)
                    if u == TG - 1 and real(prv):
                        wait(act, att_done, at(prv, 1, 1))
                        wait(act, yt_done, at(prv, 1, -1))
                        nc.scalar.activation(ys[:, prv[1] % 2, :], attb[:], ACT.Identity, scale=1.0 / (XS * WS), bias=ybias[:, 0:1]).then_inc(y_ready, 1)
                    if is_step(g, NG) and u in (2, 3):
                        spread_out(first, 2 * (u - 2))
                        spread_out(first, 2 * (u - 2) + 1)
            steps(act, body, -1, NG)

            def experts(g):
                nxt = sh(g, 1)
                for j in range(CH // 2):
                    if is_step(g, 1) and j == 3:
                        act.wait_ge(sq_in, 5)
                        nc.scalar.sqrt(vb[:, N2:], va[:, N2:]).then_inc(sq_done, 1)
                    if real(g):
                        for c in (2 * j, 2 * j + 1):
                            e, k = expert(c)
                            wait(act, h_done, at(g, CH, c + 1))
                            wait(act, ffn2_done, at(g, CH // 2, (c - 4) // 2 + 1))
                            nc.scalar.activation(hh[:, c % 4], hidb[c % 4][:], ACT.Gelu, scale=1.0 / (XS * WS),
                                                 bias=cols[:, 2 * e + k:2 * e + k + 1]).then_inc(gelu_ready, 1)
                    if j == 3 and real(nxt):
                        gate_tanh(nxt)
                    if j == 5 and real(nxt):
                        weights_out(nxt)
                    if j in (6, 7) and real(nxt):
                        spread_out(nxt, 2 * (j - 6))
                        spread_out(nxt, 2 * (j - 6) + 1)
            steps(act, experts, 0, NG - 1)

        @block.vector
        def _(dve):
            n = [0]

            def link(ins):
                n[0] += 1
                ins.then_inc(dve_step, 1)
                dve.wait_ge(dve_step, n[0])

            def variance(eps, lo, hi):
                me, qe, mo, qo = (st[:, lo:hi, k] for k in (1, 2, 4, 5))
                m, a, b_, v = (t[:, lo:hi] for t in (mean, va, vb, vc))
                link(nc.vector.tensor_tensor(m, me, mo, ALU.add))
                link(nc.vector.tensor_tensor(a, me, mo, ALU.subtract))
                link(nc.vector.tensor_tensor(b_, qe, qo, ALU.add))
                link(nc.vector.tensor_scalar(m, m, 0.5, None, ALU.mult))
                link(nc.vector.tensor_tensor(a, a, a, ALU.mult))
                link(nc.vector.tensor_scalar(b_, b_, 1.0 / C, eps, ALU.mult, ALU.add))
                link(nc.vector.scalar_tensor_tensor(v, a, 0.25, b_, ALU.mult, ALU.add))
                nc.vector.tensor_copy(a, v).then_inc(sq_in, 1)

            def rsqrt(count, lo, hi):
                r, a, b_, v = (t[:, lo:hi] for t in (rstd, va, vb, vc))
                dve.wait_ge(sq_done, count)
                link(nc.vector.reciprocal(r, b_))
                link(nc.vector.tensor_tensor(b_, r, r, ALU.mult))
                link(nc.vector.tensor_tensor(a, b_, v, ALU.mult))
                link(nc.vector.tensor_scalar(a, a, -0.5 * XS, 1.5 * XS, ALU.mult, ALU.add))
                nc.vector.tensor_tensor(r, r, a, ALU.mult).then_inc(rstd_ready, 1)
                dve.wait_ge(rstd_ready, count)

            def statistics(lo, hi):
                dve.wait_ge(x_in[max(k for k in range(len(x_in)) if LOADS[k] <= lo)], 16)
                for v in range(lo, hi):
                    nc.vector.bn_stats(st[:, v, :], x_sb[:, v, :]).then_inc(stats1_ready, 1)

            def split_g():
                dve.wait_ge(g_done, 1)
                link(nc.vector.tensor_scalar(g32[:], banks[4][:], WS, None, ALU.mult))
                link(nc.vector.tensor_copy(g_hi[:], g32[:]))
                nc.vector.tensor_tensor(g_lo[:], g32[:], g_hi[:], ALU.subtract).then_inc(g_ready, 1)

            dve.wait_ge(ident_ready, 2)
            nc.vector.tensor_reduce(par[:], ident[:].rearrange("p (a n c) -> p n a c", n=2, c=WSZ), axis=AX.XY,
                                    op=ALU.add).then_inc(par_ready, 1)
            dve.wait_ge(wT_done, 1)
            nc.vector.tensor_copy(wkT[:], banks[1][0:DK, :].rearrange("p (h c) -> p h c", h=HEADS)).then_inc(qk_ready, 1)
            statistics(0, QT // 2)
            dve.wait_ge(stats1_ready, QT // 2)
            variance(EPS_C, 0, QT // 2)
            rsqrt(1, 0, QT // 2)

            def normalise(g, src, hb):
                b = g[1] % 2
                for v in range(TG):
                    ins = nc.vector.tensor_scalar(xn[:, b, v], src[:, idx(g, TG, v), :], mean[:, bass.ds(idx(g, TG, v), 1)],
                                                  rstd[:, bass.ds(idx(g, TG, v), 1)], ALU.subtract, ALU.mult)
                ins.then_inc(half_ready, 1)
                wait(dve, half_ready, at(g, 2, hb + 1))
                nc.vector.tensor_copy(hl[:, b, :, 0, :], xn[:, b]).then_inc(half_ready, 1)
                wait(dve, half_ready, at(g, 2, hb + 2))
                nc.vector.tensor_tensor(hl[:, b, :, 1, :], xn[:, b], hl[:, b, :, 0, :],
                                        ALU.subtract).then_inc(norm_ready, 1)

            def gate(t, residual_high=None):
                b = t[1] % 2
                done = [0]

                def step(ins):
                    done[0] += 1
                    ins.then_inc(gate_step, 1)

                def after():
                    wait(dve, gate_step, at(t, GATE, done[0]))
                gl = ring[1][:, 0:TG * 2 * E].rearrange("p (t k e) -> p t k e", t=TG, k=2)
                wait(dve, gate_done, at(t, 1, 1))
                step(nc.vector.scalar_tensor_tensor(lg[:, b], gl[:, :, 0], 1.0 / (XS * WS),
                                                    bg_sb[:].unsqueeze(1).broadcast_to([P, TG, E]), ALU.mult, ALU.add))
                after()
                step(nc.vector.scalar_tensor_tensor(lg[:, b], gl[:, :, 1], 1.0 / (XS * WS), lg[:, b], ALU.mult, ALU.add))
                after()
                if residual_high:
                    residual_high()
                for v in range(TG):
                    step(nc.vector.max(top[:, b, v], lg[:, b, v]))
                after()
                step(nc.vector.tensor_tensor(gap[:, b], top[:, b, :, 1], top[:, b, :, 0], ALU.subtract))
                for v in range(TG):
                    step(nc.vector.max_index(topi[:, b, v], top[:, b, v], lg[:, b, v]))
                after()
                step(nc.vector.tensor_copy(topf[:, b], topi[:, b, :, 0:2]))
                after()
                for k in range(2):
                    step(nc.vector.tensor_tensor(oh[:, b, k], iota8[:].unsqueeze(1).broadcast_to([P, TG, E]),
                                                 topf[:, b, :, k].unsqueeze(2).broadcast_to([P, TG, E]), ALU.is_equal))
                wait(dve, tanh_ready, at(t, 1, 1))
                for k in range(2):
                    step(nc.vector.tensor_scalar(w12[:, b, :, k], th[:, b], (-0.5, 0.5)[k], 0.5, ALU.mult, ALU.add))
                after()
                for k in range(2):
                    step(nc.vector.tensor_tensor(oh[:, b, k], oh[:, b, k],
                                                 w12[:, b, :, k].unsqueeze(2).broadcast_to([P, TG, E]), ALU.mult))
                after()
                step(nc.vector.tensor_tensor(wd[:, b], oh[:, b, 0], oh[:, b, 1], ALU.add))
                after()
                wait(dve, wt_done, at(t, 1, -1))
                step(nc.vector.tensor_copy(wdh[:, b, :, 0], wd[:, b]))
                after()
                step(nc.vector.tensor_tensor(wdh[:, b, :, 1], wd[:, b], wdh[:, b, :, 0], ALU.subtract))
                assert done[0] == GATE

            def second_xs(t):
                wait(dve, xt2_done, at(t, 1, 1))
                wait(dve, h_done, at(t, CH, -CH))
                nc.vector.tensor_copy(xs2[:, t[1] % 2], half(ring[0])).then_inc(xs2_ready, 1)

            first, second = (None, 0), (None, 1)

            def body(g):
                nxt, prv2, nn = sh(g, 1), sh(g, -2), sh(g, 2)
                if is_step(g, -1):
                    split_g()
                    dve.wait_ge(wvo_done, 1)
                    nc.vector.tensor_scalar(wvo[:], banks[0][:, 0:PAIRS * C].rearrange("p (a c) -> p a c", a=PAIRS),
                                            WS, None, ALU.mult).then_inc(wvo_ready, 1)
                if is_step(g, 3):
                    dve.wait_ge(ffn_in, 16 * 6)
                    link(nc.vector.tensor_scalar(wg_sb[:], wg_sb[:], WS, None, ALU.mult))
                    link(nc.vector.tensor_copy(wg_hl[:, 0], wg_sb[:]))
                    nc.vector.tensor_tensor(wg_hl[:, 1], wg_sb[:], wg_hl[:, 0], ALU.subtract).then_inc(gatew_ready, 1)
                    dve.wait_ge(ident_ready, 3)
                    nc.vector.tensor_tensor(
                        sel[:].rearrange("k p (e c) -> k (p e) c", e=2),
                        ident[0:2 * E, 0:E].unsqueeze(2).broadcast_to([2 * E, E, C]),
                        ident[0:2 * E, E:2 * E].unsqueeze(2).broadcast_to([2 * E, E, C]), ALU.add).then_inc(gatew_ready, 1)
                for u in range(TG):
                    t, v = tile(g, u)
                    if real(t):
                        src = dots[v % 2][:].rearrange("p (h j) -> p h j", h=HEADS)
                        wait(dve, dots_done, at(t, TG, v + 1))
                        nc.vector.tensor_reduce(mx[:, v % 2], src, axis=AX.X, op=ALU.max).then_inc(mx_ready, 1)
                        wait(dve, mx_ready, at(t, TG, v + 1))
                        wait(dve, exp_ready, at(t, TG, v - 1))
                        nc.vector.tensor_tensor(sc[:, v % 2], src, mx[:, v % 2].unsqueeze(2).broadcast_to([P, HEADS, WT]),
                                                ALU.subtract).then_inc(sub_ready, 1)
                    t, v = tile(g, u - 1)
                    if real(t):
                        wait(dve, exp_ready, at(t, TG, v + 1))
                        nc.vector.reduce_sum(sm[:, v % 2], pe_[:, v % 2], axis=AX.X).then_inc(sum_ready, 1)
                        wait(dve, sum_ready, at(t, TG, v + 1))
                        wait(dve, pn_ready, at(t, TG, v - 1))
                        nc.vector.reciprocal(rs[:, v % 2], sm[:, v % 2]).then_inc(rs_ready, 1)
                    if u == 1 and real(nxt):
                        b = nxt[1] % 2
                        src = turn[XT][:].rearrange("p (t y n c) -> p t y n c", t=TG, y=WSZ, n=2)
                        dst = bd[:, b].rearrange("p (t n) k (y c) -> p t y n k c", n=2, y=WSZ)
                        wait(dve, xt_done, at(nxt, 1, 1))
                        wait(dve, dots_done, at(nxt, TG, -TG))
                        if is_step(nxt, 0):
                            dve.wait_ge(zeroed, 2)
                        for k in range(2):
                            nc.vector.tensor_copy(dst[k * C:(k + 1) * C, :, :, :, k, :], src[k * C:(k + 1) * C]).then_inc(bd_ready, 1)
                    if u == 2 and real(prv2):
                        src = turn[YT][:].rearrange("p (t k c) -> p t k c", t=TG, k=2)
                        b = prv2[1] % 2
                        wait(dve, yt_done, at(prv2, 1, 1))
                        xs = x_sb[:, bass.ds(idx(prv2, TG), TG), :]
                        xd = x1[:, bass.ds(idx(prv2, TG), TG), :]
                        nc.vector.tensor_tensor(tmp[:, b], src[:, :, 0], xs, ALU.add).then_inc(x1_ready, 1)
                        wait(dve, x1_ready, at(prv2, 2, 1))
                        nc.vector.tensor_tensor(xd, src[:, :, 1], tmp[:, b], ALU.add).then_inc(x1_ready, 1)
                        wait(dve, x1_ready, at(prv2, 2, 2))
                        for v in range(TG):
                            ins = nc.vector.bn_stats(st[:, idx(prv2, TG, v), :], x1[:, idx(prv2, TG, v), :])
                        ins.then_inc(stats2_ready, 1)
                    if is_step(g, 0) and u == 0:
                        link(nc.vector.memset(ybias[:], 0.0))
                        dve.wait_ge(ybias_done, 1)
                        dve.wait_ge(cols_ready, 1)
                        nc.vector.tensor_tensor(ybias[0:C, :], banks[1][0:C, 256:257], cols[0:C, 22:23], ALU.add).then_inc(ybias_ready, 1)
                    if u == 0 and real(g):
                        wait(dve, z_done, at(g, TG, -TG))
                        if is_step(g, 0):
                            dve.wait_ge(par_ready, 1)
                        for swapped in range(2):
                            if swapped:
                                wait(dve, xswap_done, at(g, 1, 1))
                                src = turn[XSWAP][:, 0:TG * C].rearrange("p (t c) -> p t c", t=TG)
                            else:
                                src = xn[:, g[1] % 2]
                            for w in range(2):
                                k = w ^ swapped
                                dst = bt[:, g[1] % 2].rearrange("p (t n) j -> p t n j", n=2)
                                nc.vector.tensor_scalar(dst[:, :, w, k * C:(k + 1) * C], src, par[:, k:k + 1], None,
                                                        ALU.mult).then_inc(bt_ready, 1)
                    if is_step(g, -1) and u == 3:
                        dve.wait_ge(cols_done, 1)
                        nc.vector.tensor_copy(cols[:], banks[1][:, 0:23]).then_inc(cols_ready, 1)
                    if is_step(g, 0) and u == 3:
                        dve.wait_ge(cw_ready, 2)
                        cvt = cv32[:].rearrange("p (t c) -> p t c", t=TAPS)
                        nc.vector.tensor_copy(cv[0:C, :, 0, :], cvt).then_inc(cv_ready, 1)
                        dve.wait_ge(cv_ready, 1)
                        nc.vector.tensor_tensor(cv[0:C, :, 1, :], cvt, cv[0:C, :, 0, :], ALU.subtract).then_inc(cv_ready, 1)
                    if is_step(g, 3):
                        dve.wait_ge(w1_high, u + 1)
                        nc.vector.scalar_tensor_tensor(w1_lo[:, w1_part(u)], w1_sb[:, w1_part(u)], WS, w1_hi[:, w1_part(u)],
                                                       ALU.mult, ALU.subtract).then_inc(w1_ready, 1)
                    if is_step(g, -1) and u == 1:
                        statistics(QT // 2, QT)
                        dve.wait_ge(stats1_ready, QT)
                        variance(EPS_C, QT // 2, QT)
                    if is_step(g, 0) and u in (1, 2):
                        statistics(QT + (u - 1) * QT // 2, QT + u * QT // 2)
                    if is_step(g, 1):
                        statistics(QT + (u + 2) * QT // 2, QT + (u + 3) * QT // 2)
                    if is_step(g, 2) and u == 0:
                        dve.wait_ge(stats1_ready, NT)
                        variance(EPS_C, QT, NT)
                    if is_step(g, 2) and u == 2:
                        rsqrt(3, QT, NT)
                    if is_step(g, NG - 2) and u == 0:
                        dve.wait_ge(stats2_ready, N2 // TG)
                        variance(EPS_T, 0, N2)
                    if is_step(g, NG - 2) and u == 2:
                        rsqrt(4, 0, N2)
                    if is_step(g, NG - 1):
                        if u == 1:
                            normalise(first, x1, 2 * NG)
                        if u == 3:
                            second_xs(first)
                            normalise(second, x1, 2 * NG)
                    if is_step(g, NG) and u == 0:
                        gate(first)
                    if u == 3 and real(nn) and g[0] is None and g[1] < 0:
                        normalise(nn, x_sb, 0)
                    if is_step(g, -1) and u == 3:
                        rsqrt(2, QT // 2, QT)
            steps(dve, body, -2, NG + 1)

            def experts(g):
                nxt, nn, prv = sh(g, 1), sh(g, 2), sh(g, -1)
                if is_step(g, 1):
                    dve.wait_ge(stats2_ready, NG)
                    variance(EPS_T, N2, NT)

                def pair_out(t, p):
                    wait(dve, ffn2_done, at(t, CH // 2, 2 * p + 2))
                    wait(dve, wb_ready, at(t, EP, p + 1))
                    wait(dve, acc_ready, at(t, 3, (-2, -2, -1, 0)[p]))
                    nc.vector.scalar_tensor_tensor(yw[:, p], outb[p % 2][:], cols[:, 16 + p:17 + p], wb[:, t[1] % 2, p],
                                                   ALU.add, ALU.mult).then_inc(yw_ready, 1)

                halves = ring[0][:].rearrange("p (t k c) -> p t k c", t=TG, k=2)

                def residual_high():
                    wait(dve, f_done, at(prv, 1, 1))
                    nc.vector.tensor_tensor(tmp[:, prv[1] % 2], halves[:, :, 0], x1[:, bass.ds(idx(prv, TG), TG), :],
                                            ALU.add).then_inc(o_step, 1)

                for j in range(CH // 2):
                    if j == 0:
                        if real(prv):
                            pair_out(prv, 3)
                        if real(nxt):
                            second_xs(nxt)
                    if j in (2, 4, 6) and real(g):
                        pair_out(g, j // 2 - 1)
                    if is_step(g, 1) and j == 7:
                        rsqrt(5, N2, NT)
                    if j == 3:
                        if real(nxt):
                            gate(nxt, residual_high if real(prv) else None)
                        elif real(prv):
                            residual_high()
                        if real(prv):
                            b = prv[1] % 2
                            wait(dve, stored[b], at(sh(prv, -b), 8, 0))
                            wait(dve, o_step, at(prv, 1, 1))
                            nc.vector.tensor_tensor(ob[:, b], halves[:, :, 1], tmp[:, b], ALU.add).then_inc(out_ready, 1)
                    if j == 7 and real(nn):
                        wait(dve, xt2_done, at(nn, 1, -1))
                        normalise(nn, x1, 2 * NG)
            steps(dve, experts, 0, NG)

        @block.tensor
        def _(pe):
            pe.wait_ge(ident_ready, 2)
            pe.wait_ge(wqk_in, 32)
            for bank, w in ((banks[0], wq_sb), (banks[1], wk_sb), (banks[2], wv_sb)):
                if w is wv_sb:
                    pe.wait_ge(wv_in, 16)
                for h in range(HEADS):
                    last = nc.tensor.transpose(bank[0:DK, h * C:(h + 1) * C], w[:, h * DK:(h + 1) * DK], ident[0:C, 0:C])
                if w is wk_sb:
                    last.then_inc(wT_done, 1)
            for k in range(2):
                last = nc.tensor.transpose(banks[3][:, k * C:(k + 1) * C], wv_sb[:, k * P:(k + 1) * P], ident[0:C, 0:C])
            last.then_inc(wT_done, 1)
            pe.wait_ge(qk_ready, 2)
            for h in range(HEADS):
                last = nc.tensor.matmul(banks[4][:, h * C:(h + 1) * C], wqT[:, h].rearrange("p a c -> p (a c)"), wkT[:, h],
                                        start=True, stop=True)
            last.then_inc(g_done, 1)
            pe.wait_ge(v_ready, 2)
            pe.wait_ge(ident_ready, 7)
            pe.wait_ge(wout_in, 32)
            for h in range(HEADS):
                o = (h % 2) * C
                last = nc.tensor.matmul(banks[0][o:o + C, (h // 2) * C:(h // 2 + 1) * C], wvTh[:, h], wo_h[:, h],
                                        start=True, stop=True)
            last.then_inc(wvo_done, 1)

            def conv_weights(u):
                if u == 0:
                    pe.wait_ge(wloc_in, 32)
                    for j in range(2):
                        for hf in range(2):
                            for ic in range(2):
                                last = nc.tensor.matmul(vlb[j][hf * C:(hf + 1) * C, :], wvT[:, ic],
                                                        wloc[:, ic, 4 * j + hf:4 * j + hf + 3:2, :], start=(ic == 0), stop=(ic == 1))
                        last.then_inc(vl_done, 1)
                if u == 1:
                    pe.wait_ge(vl_ready, 1)
                    for ic in range(2):
                        last = nc.tensor.matmul(vlb[2][0:C, 0:HC], wvT[:, ic], wloc[:, ic, TAPS - 1], start=(ic == 0), stop=(ic == 1))
                    last.then_inc(vl_done, 1)
                for j in range(3):
                    if (j == 0 and u == 1) or (j > 0 and u == 2):
                        pe.wait_ge(vl_ready, min(j + 2, 3))
                        if j == 2:
                            pe.wait_ge(vlT_ready, 1)
                        for m in range(2 * j, min(2 * j + 2, TP)):
                            n = P if m < TP - 1 else C
                            for k in range(2):
                                o = (m % 2) * 2 * P + k * n
                                last = nc.tensor.transpose(vltb[j][:, o:o + n], vl[0:n, m, k * P:(k + 1) * P], ident[0:n, 0:n])
                        last.then_inc(vlT_done, 1)
                if u == 3:
                    pe.wait_ge(vlT_ready, 3)
                    for k in [TAPS - 1] + list(range(TAPS - 1)):
                        for oc in range(2):
                            last = nc.tensor.matmul(banks[4 if k < 8 else 3][0:C, (k % 8) * C:(k % 8 + 1) * C],
                                                    vlT[:, k // 2, oc, (k % 2) * C:(k % 2 + 1) * C], wo_sb[:, oc],
                                                    start=(oc == 0), stop=(oc == 1))
                        if k >= 7:
                            last.then_inc(cw_done, 1)
                    pe.wait_ge(cw_ready, 1)

            def do_a(nxt, pr):
                b = nxt[1] % 2
                bank = turn[a_turn[pr]]
                rhs = xsp[:, b, :, 1:1 + HI, 1:1 + WI]
                for hv, wsp in enumerate((g_hi, g_lo)):
                    last = nc.tensor.matmul(bank[:], wsp[:, pr * P:(pr + 1) * P], rhs, start=(hv == 0), stop=(hv == 1))
                last.then_inc(a_done, 1)

            def second_xt(t):
                wait(pe, norm_ready, at(t, 1, NG + 1))
                wait(pe, wb_ready, at(t, EP, -1))
                for k in range(TG):
                    last = nc.tensor.transpose(half(ring[0])[:, k * P:(k + 1) * P],
                                               hl[:, t[1] % 2, k].rearrange("p a c -> p (a c)"), ident16[:])
                last.then_inc(xt2_done, 1)

            def gate_logits(t):
                wait(pe, xs2_ready, at(t, 1, 1))
                wait(pe, wb_ready, at(t, EP, 0))
                for v in range(TG):
                    last = nc.tensor.matmul(ring[1][:, v * 2 * E:(v + 1) * 2 * E], xs2[:, t[1] % 2, v * P:(v + 1) * P],
                                            wg_hl[:].rearrange("p k e -> p (k e)"), start=True, stop=True)
                last.then_inc(gate_done, 1)

            def weights_t(t):
                wait(pe, gate_step, at(t, GATE, GATE))
                for k in range(TG):
                    last = nc.tensor.transpose(half(ring[1])[0:2 * E, k * P:(k + 1) * P],
                                               wdh[:, t[1] % 2, k].rearrange("p a e -> p (a e)"), ident16[:])
                last.then_inc(wt_done, 1)

            def spread(t, p):
                wait(pe, wt_ready, at(t, 1, 1))
                if p == 0:
                    wait(pe, out_ready, at(sh(t, -2), 1, 1))
                wait(pe, wb_ready, at(t, EP, p - 1))
                nc.tensor.matmul(ring[p % 2][:], sel[:, p], wdT[:, t[1] % 2], start=True, stop=True).then_inc(wb_done, 1)

            first = (None, 0)

            def body(g):
                nxt, prv, prv2 = sh(g, 1), sh(g, -1), sh(g, -2)
                for u in range(TG):
                    t, v = tile(g, u)
                    if real(t):
                        b = t[1] % 2
                        if v == 0:
                            wait(pe, a_ready, at(t, PAIRS, PAIRS))
                            wait(pe, bd_ready, at(t, 2, 2))
                        wait(pe, sub_ready, at(t, TG, v - 1))
                        if is_step(t, 0) and v == 1:
                            pe.wait_ge(ybias_ready, 1)
                        for pr in range(PAIRS):
                            for w in range(2):
                                last = nc.tensor.matmul(
                                    dots[v % 2][w * WT:(w + 1) * WT, pr * P:(pr + 1) * P],
                                    aa[:, b, pr, w * TG * WT + v * WT:w * TG * WT + (v + 1) * WT],
                                    bd[:, b, 2 * v + w].rearrange("p a j -> p (a j)"), start=True, stop=True)
                        last.then_inc(dots_done, 1)
                    nb = nxt[1] % 2
                    if u == 0 and real(g):
                        wait(pe, a_ready, at(g, PAIRS, 3))
                        for hv in range(2):
                            last = nc.tensor.matmul(turn[XSWAP][:, 0:TG * C], swap16[:], hl[:, g[1] % 2, :, hv, :],
                                                    start=(hv == 0), stop=(hv == 1))
                        last.then_inc(xswap_done, 1)
                    if u == 1:
                        if real(prv):
                            wait(pe, y_ready, at(prv, 1, 0))
                            if is_step(prv, 0):
                                pe.wait_ge(cv_in, 16)
                            for k in range(TAPS):
                                rhs = xsp[:, prv[1] % 2, :, k // 3:k // 3 + HI, k % 3:k % 3 + WI]
                                last = nc.tensor.matmul(attb[:], cv[:, k].rearrange("p a c -> p (a c)"), rhs,
                                                        start=(k == 0), stop=False, skip_group_check=True)
                            last.then_inc(conv_done, 1)
                        if real(nxt):
                            wait(pe, norm_ready, at(nxt, 1, 1))
                            wait(pe, a_ready, at(nxt, PAIRS, 0))
                            for k in range(TG):
                                last = nc.tensor.transpose(half(turn[X16])[:, k * P:(k + 1) * P],
                                                           hl[:, nb, k].rearrange("p a c -> p (a c)"), ident16[:])
                            last.then_inc(x16_done, 1)
                    if u == 2:
                        if real(nxt):
                            if is_step(nxt, 0):
                                pe.wait_ge(g_ready, 1)
                            wait(pe, xsp_ready, at(nxt, 1, 1))
                            wait(pe, bt_ready, at(nxt, 4, 0))
                            do_a(nxt, 0)
                            do_a(nxt, 1)
                        if real(prv2):
                            if real(nxt):
                                wait(pe, bd_ready, at(nxt, 2, 2))
                            else:
                                wait(pe, bd_ready, 2 * NG)
                                wait(pe, x1_ready, at(prv2, 2, 0))
                            wait(pe, y_ready, at(prv2, 1, 1))
                            for k in range(TG):
                                last = nc.tensor.transpose(turn[YT][:, k * P:(k + 1) * P], ys[:, prv2[1] % 2, k * P:(k + 1) * P], ident[:])
                            last.then_inc(yt_done, 1)
                    if is_step(g, NG - 1) and u == 3:
                        pe.wait_ge(bt_ready, 4 * NG)
                        second_xt(first)
                    if is_step(g, NG) and u == 0:
                        pe.wait_ge(gatew_ready, 2)
                        gate_logits(first)
                    if is_step(g, NG) and u == 2:
                        weights_t(first)
                    if u == 3:
                        if real(nxt):
                            wait(pe, a_ready, at(nxt, PAIRS, 1))
                            do_a(nxt, 2)
                            wait(pe, a_ready, at(nxt, PAIRS, 2))
                            do_a(nxt, 3)
                        if real(prv):
                            wait(pe, z_ready, at(prv, TG, TG))
                            for k in range(2):
                                for hf in range(2):
                                    pr = 2 * hf + k
                                    last = nc.tensor.matmul(attb[hf * C:(hf + 1) * C, :], wvo[:, pr], zs[:, prv[1] % 2, :, pr, :],
                                                            start=False, stop=(k == 1), skip_group_check=True)
                            last.then_inc(att_done, 1)
                    if is_step(g, -1) and u == 3:
                        pe.wait_ge(rows_in, 16 * 5)
                        nc.tensor.transpose(banks[1][:, 0:23], rows[:], ident[0:23, 0:23]).then_inc(cols_done, 1)
                    if is_step(g, 0):
                        if u == 0:
                            pe.wait_ge(cols_ready, 1)
                            for k in range(2):
                                last = nc.tensor.matmul(banks[1][0:C, 256:257], wo_sb[:, k], cols[:, 20 + k:21 + k],
                                                        start=(k == 0), stop=(k == 1))
                            last.then_inc(ybias_done, 1)
                        conv_weights(u)
                    t, v = tile(g, u - 2)
                    if real(t):
                        wait(pe, pn_ready, at(t, TG, v + 1))
                        wait(pe, pt_ready, at(t, TG, v))
                        for pr in range(PAIRS):
                            last = nc.tensor.transpose(ptb[:, pr * P:(pr + 1) * P], pn[:, v % 2, pr * P:(pr + 1) * P], ident[:])
                        last.then_inc(pt_done, 1)
                    t, v = tile(g, u - 3)
                    if real(t):
                        wait(pe, pt_ready, at(t, TG, v + 1))
                        wait(pe, bt_ready, at(t, 4, 4))
                        wait(pe, z_ready, at(t, TG, v))
                        zo = zb[:].rearrange("p (a y n c) -> p a y n c", a=PAIRS, y=WSZ, n=2)
                        for w in range(2):
                            last = nc.tensor.matmul(zo[:, :, :, w, :], bt[:, t[1] % 2, 2 * v + w],
                                                    pt[:, v % 2, :, w * WT:(w + 1) * WT], start=True, stop=True)
                        last.then_inc(z_done, 1)
                    if u == 1 and real(nxt):
                        wait(pe, xsp_ready, at(nxt, 1, 1))
                        if real(sh(g, -3)):
                            wait(pe, x1_ready, at(sh(g, -3), 2, 2))
                        nc.tensor.matmul(turn[XT][:], both16[:].rearrange("p k c -> p (k c)"), xsp[:, nb, :, 1:1 + HI, 1:1 + WI],
                                         start=True, stop=True).then_inc(xt_done, 1)
                    if is_step(g, NG) and u in (2, 3):
                        spread(first, 2 * (u - 2))
                        spread(first, 2 * (u - 2) + 1)
            steps(pe, body, -1, NG + 1)

            pe.wait_ge(w1_ready, 4)

            def experts(g):
                nxt, prv = sh(g, 1), sh(g, -1)

                def ffn2(t, j):
                    for c in (2 * j, 2 * j + 1):
                        e, k = expert(c)
                        hf = (e % 2) * C
                        wait(pe, gelu_ready, at(t, CH, c + 1))
                        if k == 0 and c % 2 == 0:
                            wait(pe, yw_ready, at(t, EP, c // 4 - 1))
                        last = nc.tensor.matmul(outb[(c // 4) % 2][hf:hf + C, :], w2_sb[:, e, k], hh[:, c % 4],
                                                start=(k == 0), stop=(k == 1))
                    last.then_inc(ffn2_done, 1)

                for j in range(CH // 2):
                    if real(g):
                        for c in (2 * j, 2 * j + 1):
                            e, k = expert(c)
                            if c == 0:
                                wait(pe, xs2_ready, at(g, 1, 1))
                            wait(pe, gelu_ready, at(g, CH, c - 3))
                            o = (2 * e + k) * P
                            nc.tensor.matmul(hidb[c % 4][:], w1_hi[:, o:o + P], xs2[:, g[1] % 2], start=True, stop=False)
                            nc.tensor.matmul(hidb[c % 4][:], w1_lo[:, o:o + P], xs2[:, g[1] % 2], start=False,
                                             stop=True).then_inc(h_done, 1)
                    if j == 0 and real(prv):
                        ffn2(prv, CH // 2 - 1)
                    if j > 0 and real(g):
                        ffn2(g, j - 1)
                    if j == 0 and real(nxt):
                        second_xt(nxt)
                    if j == 1 and real(nxt):
                        gate_logits(nxt)
                    if j == 3 and real(prv):
                        wait(pe, acc_ready, at(prv, 3, 3))
                        if not real(nxt):
                            wait(pe, out_ready, at(prv, 1, 0))
                            wait(pe, wb_ready, EP * NG)
                        for k in range(TG):
                            last = nc.tensor.transpose(ring[0][:, k * P:(k + 1) * P], acc[:, prv[1] % 2, k * P:(k + 1) * P], ident[:])
                        last.then_inc(f_done, 1)
                    if j == 5 and real(nxt):
                        weights_t(nxt)
                    if j in (6, 7) and real(nxt):
                        spread(nxt, 2 * (j - 6))
                        spread(nxt, 2 * (j - 6) + 1)
            steps(pe, experts, 0, NG)


_INS = ['x', 'L0_conv_w_q', 'L0_conv_w_k', 'L0_conv_w_v', 'L0_conv_w_local', 'L0_conv_b_local', 'L0_conv_w_out',
        'L0_conv_b_out', 'L0_ffn_Wg', 'L0_ffn_bg', 'L0_ffn_W1', 'L0_ffn_b1', 'L0_ffn_W2', 'L0_ffn_b2']


def kernel(**inputs):
    import concourse.bacc as bacc
    from concourse.bass_utils import run_bass_kernel_spmd

    nc = bacc.Bacc("TRN2", target_bir_lowering=False, num_devices=1)
    arrays, args = {}, []
    for name in _INS:
        a = np.ascontiguousarray(inputs[name])
        if name == 'x':
            a = a.reshape(B * HI * WI, C)
        arrays[f"in_{name}"] = a
        args.append(nc.dram_tensor(f"in_{name}", a.shape, mybir.dt.from_np(a.dtype), kind="ExternalInput").ap())
    args.append(nc.dram_tensor("out", (B * HI * WI, C), F32, kind="ExternalOutput").ap())
    program(nc, *args)
    r = run_bass_kernel_spmd(nc, [arrays], core_ids=[0])
    return r.results[0]["out"].reshape(B, HI, WI, C)
```
